# Optimizing a Trainium2 kernel written in Bass

```python
import numpy as np
import jax
import jax.numpy as jnp

def _softmax(x, axis=-1):
    return jax.nn.softmax(x, axis=axis)

def _gelu(x):
    return jax.nn.gelu(x, approximate=True)

def _silu(x):
    return jax.nn.silu(x)

def _sigmoid(x):
    return jax.nn.sigmoid(x)

def _layernorm(x, axis=-1, eps=1e-05):
    m = jnp.mean(x, axis=axis, keepdims=True)
    v = jnp.var(x, axis=axis, keepdims=True)
    return (x - m) / jnp.sqrt(v + eps)

def _scatter_add(tgt, idx, src, axis=0):
    return tgt.at[idx].add(src)

def _segment_sum(src, seg, n):
    return jax.ops.segment_sum(src, seg, n)
kernel_name = 'mk_adj_resnorm_d2_adj_r2_625ab3'

def setup_inputs(seed: int=0):
    np.random.seed(seed)
    _w = jnp.asarray

    def _rec_inputs():
        import jax
        import jax.numpy as jnp
        _gk = jax.random.key(seed)
        x = 7.22e-05 + 1 * jax.random.normal(jax.random.fold_in(_gk, 1), (8, 1024, 256), jnp.float32)
        _a = jax.random.bernoulli(jax.random.fold_in(_gk, 2), 0.015625, (8, 1024, 1024))
        _a = jnp.logical_or(_a, jnp.swapaxes(_a, -1, -2))
        _a = jnp.logical_or(_a, jnp.eye(1024, dtype=bool))
        _af = _a.astype(jnp.float32)
        _af = _af * jax.random.uniform(jax.random.fold_in(_gk, 3), (8, 1024, 1024), jnp.float32, 0.05, 1)
        adj = _af
        return (x, adj)
    x, adj = _rec_inputs()

    def _L0_gnn_setup():
        import jax, jax.numpy as jnp
        import numpy as np
        EPS_LN = 1e-05

        def hypergraph_conv(x, adj, W, b):
            N, C, _ = adj.shape
            H = (adj != 0).astype(x.dtype)
            w = adj.reshape(N, -1)[:, :C]
            xw = jnp.einsum('ncd,hd->nch', x, W)
            Dn = jnp.einsum('nce,ne->nc', H, w)
            Dn = jnp.where(Dn > 0, 1.0 / Dn, 0.0)
            Be = H.sum(axis=1)
            Be = jnp.where(Be > 0, 1.0 / Be, 0.0)
            m = Be[:, :, None] * jnp.einsum('nce,nch->neh', H, xw)
            out = Dn[:, :, None] * jnp.einsum('nce,neh->nch', H, m)
            return out + b

        def layer_norm(x, g, b):
            mu = jnp.mean(x, axis=-1, keepdims=True)
            var = jnp.var(x, axis=-1, keepdims=True)
            return (x - mu) * jax.lax.rsqrt(var + EPS_LN) * g + b
        key = jax.random.key(seed)
        ks = jax.random.split(key, 4)
        N, C, Din, Dh, Dout = (16, 512, 256, 512, 256)
        x = jax.random.normal(ks[0], (N, C, Din), dtype=jnp.float32)
        adj = jax.random.uniform(ks[1], (N, C, C), dtype=jnp.float32, minval=0.1, maxval=1.0)
        W1 = jax.random.normal(ks[2], (Dh, Din), dtype=jnp.float32) * (1.0 / np.sqrt(Din))
        b1 = jnp.zeros((Dh,), dtype=jnp.float32)
        gamma = jnp.ones((Dh,), dtype=jnp.float32)
        beta = jnp.zeros((Dh,), dtype=jnp.float32)
        W2 = jax.random.normal(ks[3], (Dout, Dh), dtype=jnp.float32) * (1.0 / np.sqrt(Dh))
        b2 = jnp.zeros((Dout,), dtype=jnp.float32)
        return {'x': x, 'adj': adj, 'W1': W1, 'b1': b1, 'gamma': gamma, 'beta': beta, 'W2': W2, 'b2': b2}
    _L0_gnn_all = _L0_gnn_setup()
    _L0_gnn_in = {k: v for k, v in _L0_gnn_all.items() if k in ('W1', 'b1', 'gamma', 'beta', 'W2', 'b2')}
    del _L0_gnn_all

    def _L1_gnn_setup():
        import jax, jax.numpy as jnp
        import numpy as np
        EPS = 1e-06
        key = jax.random.key(seed)
        k1, k2, k3 = jax.random.split(key, 3)
        B, N, F, O = (8, 2048, 256, 256)
        x = jax.random.normal(k1, (B, N, F), dtype=jnp.float32)
        adj = jax.random.uniform(k2, (B, N, N), dtype=jnp.float32)
        W = jax.random.normal(k3, (O, 2 * F), dtype=jnp.float32) * (1.0 / np.sqrt(2 * F))
        return {'x': x, 'adj': adj, 'W': W}
    _L1_gnn_all = _L1_gnn_setup()
    _L1_gnn_in = {k: v for k, v in _L1_gnn_all.items() if k in ('W',)}
    del _L1_gnn_all
    return {'x': x, 'adj': adj, 'L0_gnn_W1': _L0_gnn_in['W1'], 'L0_gnn_b1': _L0_gnn_in['b1'], 'L0_gnn_gamma': _L0_gnn_in['gamma'], 'L0_gnn_beta': _L0_gnn_in['beta'], 'L0_gnn_W2': _L0_gnn_in['W2'], 'L0_gnn_b2': _L0_gnn_in['b2'], 'L1_gnn_W': _L1_gnn_in['W']}

def reference(x, adj, L0_gnn_W1, L0_gnn_b1, L0_gnn_gamma, L0_gnn_beta, L0_gnn_W2, L0_gnn_b2, L1_gnn_W):
    import jax
    import jax.numpy as jnp

    def _L0_gnn_ref(x, adj, W1, b1, gamma, beta, W2, b2):
        import jax, jax.numpy as jnp
        import numpy as np
        EPS_LN = 1e-05

        def hypergraph_conv(x, adj, W, b):
            N, C, _ = adj.shape
            H = (adj != 0).astype(x.dtype)
            w = adj.reshape(N, -1)[:, :C]
            xw = jnp.einsum('ncd,hd->nch', x, W)
            Dn = jnp.einsum('nce,ne->nc', H, w)
            Dn = jnp.where(Dn > 0, 1.0 / Dn, 0.0)
            Be = H.sum(axis=1)
            Be = jnp.where(Be > 0, 1.0 / Be, 0.0)
            m = Be[:, :, None] * jnp.einsum('nce,nch->neh', H, xw)
            out = Dn[:, :, None] * jnp.einsum('nce,neh->nch', H, m)
            return out + b

        def layer_norm(x, g, b):
            mu = jnp.mean(x, axis=-1, keepdims=True)
            var = jnp.var(x, axis=-1, keepdims=True)
            return (x - mu) * jax.lax.rsqrt(var + EPS_LN) * g + b
        h = jax.nn.relu(hypergraph_conv(x, adj, W1, b1))
        h = layer_norm(h, gamma, beta)
        y = hypergraph_conv(h, adj, W2, b2)
        return y + x

    def _L1_gnn_ref(x, adj, W):
        import jax, jax.numpy as jnp
        import numpy as np
        EPS = 1e-06
        deg = jnp.sum(adj, axis=-1, keepdims=True)
        agg = jnp.einsum('bij,bjf->bif', adj, x) / jnp.maximum(deg, EPS)
        cat = jnp.concatenate([x, agg], axis=2)
        out = jnp.einsum('bnf,of->bno', cat, W)
        return jax.nn.relu(out)
    x = _layernorm(x + _L0_gnn_ref(x, adj, L0_gnn_W1, L0_gnn_b1, L0_gnn_gamma, L0_gnn_beta, L0_gnn_W2, L0_gnn_b2), axis=-1)
    x = _layernorm(x + _L1_gnn_ref(x, adj, L1_gnn_W), axis=-1)
    return x

_drawn_inputs = setup_inputs


def setup_inputs(seed=0):
    import zlib

    import numpy as np

    out = dict(_drawn_inputs(seed))
    spreads = {'L0_gnn_b1': (0.0, 0.1),
     'L0_gnn_gamma': (1.0, 0.2),
     'L0_gnn_beta': (0.0, 0.1),
     'L0_gnn_b2': (0.0, 0.1)}
    factors = {}
    for name, (base, spread) in spreads.items():
        noise = np.random.default_rng([zlib.crc32(name.encode()), seed]).standard_normal(out[name].shape)
        drawn = base * np.exp(spread * noise) if base else spread * noise
        out[name] = jnp.asarray(drawn.astype(out[name].dtype))
    for name, factor in factors.items():
        out[name] = (out[name] * factor).astype(out[name].dtype)
    return out
```

```python
from contextlib import ExitStack

import concourse.bass as bass
from concourse import mybir

F32 = mybir.dt.float32
F32R = mybir.dt.float32r
BF16 = mybir.dt.bfloat16
ALU = mybir.AluOpType
ACT = mybir.ActivationFunctionType

P = 128
NORM_EPS = 1e-5
DEG_EPS = 1e-6
TINY = 1.1754944e-38

PRODUCT_BANKS = {
    "S1": (0, 1, 2, 3, 4, 5, 0, 1),
    "S2": (2, 3, 4, 5),
    "P": (0, 1, 2, 0, 1, 2, 0, 1),
    "Q": (3, 4, 5, 3, 4, 5, 3, 4),
    "S3": (0, 1, 2, 5, 3, 4, 0, 1),
    "S4": (2, 5, 3, 4, 0, 1, 2, 5),
    "V": (3, 4, 0, 1, 3, 4, 0, 1),
    "L": (2, 5, 3, 4, 0, 1, 4, 5),
}
TRANSPOSE_BANKS = (6, 7)
N_BANKS = 8
GROUP = 4
LAG_T = 2
LAG_Q = 3
H_SLOTS = 3


def graph_net(nc, x, adj, W1, b1, gamma, beta, W2, b2, WL, out):
    B, C, D = x.shape
    DH = W1.shape[0]
    NT = C // P
    ND = D // P
    NH = DH // P
    CH = 512
    NCH = C // CH
    DP = D + 2
    YP = 2 * D + 1

    setup_fills = [1, 0, 0, 0, 0, 0, 3, 3]
    setup_empties = [1, 1, 1, 1, 1, 1, 3, 3]
    bank_of, nth = {}, {}
    fills = [0] * N_BANKS
    turn = [0]

    def add_job(stage, tile):
        if stage in PRODUCT_BANKS:
            bank = PRODUCT_BANKS[stage][tile]
        else:
            bank = TRANSPOSE_BANKS[turn[0] % 2]
            turn[0] += 1
        bank_of[stage, tile] = bank
        nth[stage, tile] = fills[bank]
        fills[bank] += 1

    for e in range(NT):
        add_job("S1", e)
        add_job("TA", 2 * e)
        add_job("TA", 2 * e + 1)
    for j in range(NCH * ND):
        add_job("S2", j)
    for s in range(NT + LAG_Q):
        if s < NT:
            add_job("P", s)
        if 0 <= s - LAG_T < NT:
            add_job("TH", s - LAG_T)
        if 0 <= s - LAG_Q < NT:
            add_job("Q", s - LAG_Q)
    for stage in ("S3", "S4"):
        for e in range(NT):
            add_job(stage, e)
    for i in range(NT + 1):
        if i < NT:
            add_job("TX", i)
        if i > 0:
            add_job("V", i - 1)
    for i in range(NT):
        add_job("L", i)

    ctx = ExitStack()
    with ctx:
        at = [(nc.sbuf_base + 63) // 64 * 64]

        def place(name, shape, dt, offset=None):
            n = 4 if dt != BF16 else 2
            for d in shape[1:]:
                n *= d
            if offset is None:
                offset = at[0]
                at[0] += (n + 63) // 64 * 64
            return nc.alloc_sbuf_tensor_at(name, shape, dt, offset=offset), offset, offset + (n + 63) // 64 * 64

        raw, raw_at, _ = place("raw", [P, NT, C], F32)
        H, _, _ = place("H", [P, NT, C], F32R)
        adjT, adjT_at, _ = place("adjT", [P, NT, C], F32)
        HT, HT_at, _ = place("HT", [P, NT, C], F32R)
        x_hi, _, _ = place("x_hi", [P, NT, DP], F32R)
        x_lo, _, _ = place("x_lo", [P, NT, D], F32R)
        m_hi, _, _ = place("m_hi", [P, NT, D], F32R)
        m_lo, _, _ = place("m_lo", [P, NT, D], F32R)
        x_in, _, _ = place("x_in", [P, NT, D], F32)
        xres, _, _ = place("xres", [P, NT, D], F32)
        w_row, _, _ = place("w_row", [P, C], F32)
        W1T, _, _ = place("W1T", [P, ND, DH], F32)
        gW2T, _, _ = place("gW2T", [P, NH, D], F32)
        WLT, _, _ = place("WLT", [P, ND, 2 * D], F32)
        b1_row, _, _ = place("b1_row", [P, DH], F32)
        b2_row, _, _ = place("b2_row", [P, D], F32)
        bW2_row, _, _ = place("bW2_row", [P, D], F32)
        x1T, _, _ = place("x1T", [P, 2, ND, P], F32)
        q_f32, _, _ = place("q_f32", [P, 2, D], F32)
        o_f32, _, _ = place("o_f32", [P, 2, D], F32)
        ident, _, _ = place("ident", [P, P], F32)
        small, _, _ = place("small", [P, 20, NT], F32)
        zT, _, nxt = place("zT", [P, ND, C], F32, raw_at)
        hrow, _, nxt = place("hrow", [P, H_SLOTS, DH], F32, nxt)
        xnT, _, _ = place("xnT", [P, 2, NH, P], F32, nxt)
        yv, _, nxt = place("yv", [P, NT, YP], F32, HT_at)
        unread, _, _ = place("unread", [P, C], F32, nxt)
        W1n, _, nxt = place("W1n", [P, NH, D], F32, adjT_at)
        W2n, _, nxt = place("W2n", [P, ND, DH], F32, nxt)
        WLn, _, nxt = place("WLn", [P, ND, 2 * D], F32, nxt)
        W2T, _, nxt = place("W2T", [P, NH, D], F32, nxt)
        beta_wide, _, _ = place("beta_wide", [P, NH, P], F32, nxt)

        def col(n):
            return small[:, n, :]

        (dn, dn_pos, dn_safe, dn_inv, rDn, be_safe, rBe, deg_safe, rdeg, std_h, rstd_h, std_1, rstd_1,
         std_o, rstd_o, gb) = (col(n) for n in range(16))
        gamma_c, beta_c, eps_c = gb[:, 0:NH], gb[:, NH:2 * NH], small[:, 16, 0:1]
        stats, _, _ = place("stats", [P, 3, NT, 6], F32)
        mv, _, _ = place("mv", [P, 3, NT, 2], F32)
        assert NT >= 2 * NH and at[0] <= nc.sbuf_usable_end, (at[0], nc.sbuf_usable_end)

        banks = [ctx.enter_context(nc.psum_tensor(f"bank{n}", [P, 512], F32)) for n in range(N_BANKS)]

        def sem(name):
            return ctx.enter_context(nc.semaphore(name))

        bank_full = [sem(f"bank_full{n}") for n in range(N_BANKS)]
        bank_empty = [sem(f"bank_empty{n}") for n in range(N_BANKS)]
        raw_loaded = [sem(f"raw_loaded{n}") for n in range(NT // 2)]
        x_loaded, w_loaded, weights_loaded, rows_loaded = (
            sem(n) for n in ("x_loaded", "w_loaded", "weights_loaded", "rows_loaded"))
        ident_zero, ident_ready, eps_ready, ones_ready, x_split, x_hi_done, xb_part, xb_ready = (
            sem(n) for n in ("ident_zero", "ident_ready", "eps_ready", "ones_ready", "x_split", "x_hi_done",
                             "xb_part", "xb_ready"))
        q_hi_done, q_split, y_ones = (sem(n) for n in ("q_hi_done", "q_split", "y_ones"))
        H_ready, HT_ready, dn_ready, rDn_part, rDn_ready = (
            sem(n) for n in ("H_ready", "HT_ready", "dn_ready", "rDn_part", "rDn_ready"))
        be_done, rBe_ready, m_hi_done = (sem(n) for n in ("be_done", "rBe_ready", "m_hi_done"))
        relu_done = sem("relu_done")
        deg_done, rdeg_done, o_done, sum_done = (sem(n) for n in ("deg_done", "rdeg_done", "o_done", "sum_done"))
        norms = ("h", "1", "o")
        var_done = {n: sem(f"var_done_{n}") for n in norms}
        std_done = {n: sem(f"std_done_{n}") for n in norms}
        rstd_done = {n: sem(f"rstd_done_{n}") for n in norms}
        normed = {n: sem(f"normed_{n}") for n in norms}
        W2T_scaled, beta_wide_done = sem("W2T_scaled"), sem("beta_wide_done")
        out_stored = sem("out_stored")

        def bank(stage, tile):
            return banks[bank_of[stage, tile]]

        def full(stage, tile, b):
            n = bank_of[stage, tile]
            return bank_full[n], b * fills[n] + (setup_fills[n] + nth[stage, tile] + 1)

        def emptied(stage, tile, b):
            n = bank_of[stage, tile]
            return bank_empty[n], b * fills[n] + (setup_empties[n] + nth[stage, tile] + 1)

        def free(stage, tile, b):
            n = bank_of[stage, tile]
            return bank_empty[n], b * fills[n] + (setup_empties[n] + nth[stage, tile])

        def fills_bank(ins, stage, tile):
            ins.then_inc(bank_full[bank_of[stage, tile]], 1)

        def empties_bank(ins, stage, tile):
            ins.then_inc(bank_empty[bank_of[stage, tile]], 1)

        def over_graphs(eng, graph):
            with eng.Fori(0, B - 1) as b:
                graph(b, True)
            graph(B - 1, False)

        block = ctx.enter_context(nc.Block())

        @block.sync
        def _(sp):
            def load_graph(b):
                for j in range(NT // 2):
                    sp.dma_start(raw[:, 2 * j:2 * j + 2, :],
                                 adj[b, 2 * j * P:(2 * j + 2) * P, :].rearrange("(t p) e -> p t e", p=P))\
                      .then_inc(raw_loaded[j], 16)

            def load_x(b):
                sp.dma_start(x_in[:, :, :], x[b, :, :].rearrange("(t p) d -> p t d", p=P)).then_inc(x_loaded, 16)

            def load_w(b):
                sp.dma_start(w_row[:, :], adj[b, 0, :].partition_broadcast(P)).then_inc(w_loaded, 16)

            load_x(0)
            load_w(0)
            load_graph(0)

            def graph(b, more):
                if more:
                    sp.wait_ge(dn_ready, b * NT + NT)
                    load_w(b + 1)
                    sp.wait_ge(xb_ready, b + 1)
                    sp.wait_ge(x_split, b + 1)
                    load_x(b + 1)
                    sp.wait_ge(*full("Q", NT - 1, b))
                    load_graph(b + 1)
                for j in range(NT // 2):
                    sp.wait_ge(normed["o"], b * NT + 2 * j + 2)
                    sp.dma_start(out[b, 2 * j * P:(2 * j + 2) * P, :].rearrange("(t p) d -> p t d", p=P),
                                 xres[:, 2 * j:2 * j + 2, :]).then_inc(out_stored, 16)

            over_graphs(sp, graph)
            sp.wait_ge(out_stored, 16 * (NT // 2) * B)

        @block.gpsimd
        def _(pool):
            nc.gpsimd.memset(ident[:, :], 0.0).then_inc(ident_zero, 1)
            nc.gpsimd.memset(x_hi[:, :, D:DP].bitcast(F32), 1.0).then_inc(ones_ready, 1)
            nc.gpsimd.memset(eps_c, NORM_EPS).then_inc(eps_ready, 1)
            pool.wait_ge(ident_zero, 1)
            nc.gpsimd.affine_select(out=ident[:, :], in_=ident[:, :], compare_op=ALU.not_equal, fill=1.0,
                                    base=0, pattern=[[-1, P]], channel_multiplier=1).then_inc(ident_ready, 1)

            def split_x(b):
                pool.wait_ge(x_hi_done, b + 1)
                nc.gpsimd.tensor_tensor(x_lo[:, :, :], x_in[:, :, :], x_hi[:, :, 0:D].bitcast(F32), ALU.subtract)\
                  .then_inc(x_split, 1)

            split_x(0)
            pool.wait_ge(rows_loaded, 16 * 4)

            def residual(b):
                nc.gpsimd.tensor_tensor(xres[:, :, :], x_in[:, :, :], x_in[:, :, :], ALU.add).then_inc(xb_part, 1)
                pool.wait_ge(xb_part, b + 1)
                nc.gpsimd.tensor_tensor(xres[:, :, :], xres[:, :, :],
                                        b2_row[:, :].unsqueeze(1).to_broadcast([P, NT, D]), ALU.add)\
                  .then_inc(xb_ready, 1)

            residual(0)

            def graph(b, more):
                for i in range(NT):
                    pool.wait_ge(q_hi_done, b * NT + i + 1)
                    nc.gpsimd.tensor_tensor(x_lo[:, i, :], q_f32[:, i % 2, :], x_hi[:, i, 0:D].bitcast(F32),
                                            ALU.subtract).then_inc(q_split, 1)
                if more:
                    split_x(b + 1)
                    pool.wait_ge(out_stored, b * (16 * (NT // 2)) + 16 * (NT // 2))
                    residual(b + 1)

            over_graphs(pool, graph)

        @block.scalar
        def _(act):
            for k in range(1):
                act.dma_start(W1n[:, :, :], W1.rearrange("(t p) d -> p t d", p=P)).then_inc(weights_loaded, 16)
                act.dma_start(W2n[:, :, :], W2.rearrange("(t p) d -> p t d", p=P)).then_inc(weights_loaded, 16)
                act.dma_start(WLn[:, :, :], WL.rearrange("(t p) d -> p t d", p=P)).then_inc(weights_loaded, 16)
                act.dma_start(b1_row[:, :], b1.partition_broadcast(P)).then_inc(rows_loaded, 16)
                act.dma_start(b2_row[:, :], b2.partition_broadcast(P)).then_inc(rows_loaded, 16)
                act.dma_start(gamma_c, gamma.rearrange("(k p) -> p k", p=P), allow_slow_non_contiguous=True).then_inc(rows_loaded, 16)
                act.dma_start(beta_c, beta.rearrange("(k p) -> p k", p=P), allow_slow_non_contiguous=True).then_inc(rows_loaded, 16)
            targets = [W1T[:, d, :] for d in range(ND)] + \
                      [W2T[:, 2 * k:2 * k + 2, :].rearrange("p k o -> p (k o)") for k in range(NH // 2)] + \
                      [WLT[:, d, :] for d in range(ND)]
            for n, target in enumerate(targets):
                tb = TRANSPOSE_BANKS[n % 2]
                act.wait_ge(bank_full[tb], n // 2 + 1)
                nc.scalar.activation(target, banks[tb][:, :], ACT.Copy).then_inc(bank_empty[tb], 1)

            def take_m_hi(stage, e, b, n):
                act.wait_ge(*full(stage, e, b))
                act.wait_ge(rBe_ready, b * NT + (e + 1 if stage == "S1" else NT))
                nc.scalar.activation(m_hi[:, e, :], bank(stage, e)[:, 0:D], ACT.Identity, scale=rBe[:, e:e + 1])\
                  .then_inc(m_hi_done, 1)

            def root(norm, which, std, i, b):
                act.wait_ge(var_done[norm], b * NT + i + 1)
                nc.scalar.activation(std[:, i:i + 1], mv[:, which, i, 1:2], ACT.Sqrt, bias=eps_c)\
                  .then_inc(std_done[norm], 1)

            def split_x_hi(b):
                act.wait_ge(x_loaded, b * 16 + 16)
                nc.scalar.activation(x_hi[:, :, 0:D], x_in[:, :, :], ACT.Copy).then_inc(x_hi_done, 1)

            act.wait_ge(eps_ready, 1)
            split_x_hi(0)

            def graph(b, more):
                for e in range(NT):
                    take_m_hi("S1", e, b, e)
                    for half in range(2):
                        job = 2 * e + half
                        act.wait_ge(*full("TA", job, b))
                        empties_bank(nc.scalar.activation(
                            adjT[:, half * 4:half * 4 + 4, e * P:(e + 1) * P],
                            bank("TA", job)[:, :].rearrange("p (k c) -> p k c", c=P), ACT.Copy), "TA", job)
                for j in range(NCH * ND):
                    ch, d = divmod(j, ND)
                    act.wait_ge(*full("S2", j, b))
                    empties_bank(nc.scalar.activation(zT[:, d, ch * CH:(ch + 1) * CH], bank("S2", j)[:, :],
                                                      ACT.Copy), "S2", j)
                for s in range(NT + LAG_Q):
                    if s < NT:
                        act.wait_ge(*emptied("P", s, b))
                        nc.scalar.activation(hrow[:, s % H_SLOTS, :], hrow[:, s % H_SLOTS, :], ACT.Relu)\
                          .then_inc(relu_done, 1)
                    if 0 <= s - LAG_T < NT:
                        i = s - LAG_T
                        act.wait_ge(*full("TH", i, b))
                        empties_bank(nc.scalar.activation(xnT[:, i % 2, :, :].rearrange("p k c -> p (k c)"),
                                                          bank("TH", i)[:, :], ACT.Copy), "TH", i)
                    if s < NT:
                        root("h", 0, std_h, s, b)
                    if s >= LAG_Q:
                        i = s - LAG_Q
                        act.wait_ge(*emptied("Q", i, b))
                        nc.scalar.activation(x_hi[:, i, 0:D], q_f32[:, i % 2, :], ACT.Copy).then_inc(q_hi_done, 1)
                for e in range(NT):
                    take_m_hi("S3", e, b, NT + e)
                if more:
                    split_x_hi(b + 1)
                for i in range(NT):
                    root("1", 1, std_1, i, b)
                for i in range(NT + 1):
                    if i < NT:
                        act.wait_ge(*full("TX", i, b))
                        empties_bank(nc.scalar.activation(x1T[:, i % 2, :, :].rearrange("p k c -> p (k c)"),
                                                          bank("TX", i)[:, 0:D], ACT.Copy), "TX", i)
                    if i > 0:
                        act.wait_ge(*full("V", i - 1, b))
                        empties_bank(nc.scalar.activation(yv[:, i - 1, 0:2 * D], bank("V", i - 1)[:, :], ACT.Copy),
                                     "V", i - 1)
                for i in range(NT):
                    root("o", 2, std_o, i, b)

            over_graphs(act, graph)

        @block.vector
        def _(dve):
            def build_H(b):
                dve.wait_ge(w_loaded, b * 16 + 16)
                for c in range(NT):
                    dve.wait_ge(raw_loaded[c // 2], b * 16 + 16)
                    nc.vector.tensor_scalar(H[:, c, :], raw[:, c, :], 0.0, None, ALU.not_equal).then_inc(H_ready, 1)
                    if c > 0:
                        dve.wait_ge(dn_ready, b * NT + c)
                    nc.vector.scalar_tensor_tensor(out=unread[:, :], in0=raw[:, c, :], scalar=0.0, in1=w_row[:, :],
                                                   op0=ALU.not_equal, op1=ALU.mult,
                                                   accum_out=dn[:, c:c + 1]).then_inc(dn_ready, 1)

            def moments(norm, which, src, i, b):
                nc.vector.bn_stats(stats[:, which, i, :], src)
                dve.drain()
                nc.vector.bn_aggr(mv[:, which, i, :], stats[:, which, i, :]).then_inc(var_done[norm], 1)

            def normalise(norm, which, rows, std, rstd, i, b):
                dve.wait_ge(std_done[norm], b * NT + i + 1)
                nc.vector.reciprocal(rstd[:, i:i + 1], std[:, i:i + 1]).then_inc(rstd_done[norm], 1)
                dve.wait_ge(rstd_done[norm], b * NT + i + 1)
                nc.vector.tensor_scalar(rows, rows, mv[:, which, i, 0:1], rstd[:, i:i + 1],
                                        ALU.subtract, ALU.mult).then_inc(normed[norm], 1)

            def take_m_lo(stage, e, b, n):
                dve.wait_ge(m_hi_done, b * (2 * NT) + (n + 1))
                empties_bank(nc.vector.scalar_tensor_tensor(
                    out=m_lo[:, e, :], in0=bank(stage, e)[:, 0:D], scalar=rBe[:, e:e + 1],
                    in1=m_hi[:, e, :].bitcast(F32), op0=ALU.mult, op1=ALU.subtract), stage, e)

            def build_HT(c, b):
                dve.wait_ge(*emptied("TA", 2 * c, b))
                dve.wait_ge(*emptied("TA", 2 * c + 1, b))
                nc.vector.tensor_scalar(HT[:, :, c * P:(c + 1) * P], adjT[:, :, c * P:(c + 1) * P], 0.0, None,
                                        ALU.not_equal).then_inc(HT_ready, 1)

            for n in range(1, TRANSPOSE_BANKS[0]):
                nc.vector.memset(banks[n][:, 0:1], 0.0).then_inc(bank_empty[n], 1)
            dve.wait_ge(rows_loaded, 16 * 4)
            for k in range(NH):
                nc.vector.tensor_copy(beta_wide[:, k, :], beta_c[:, k:k + 1].to_broadcast([P, P]))\
                  .then_inc(beta_wide_done, 1)
            for n in range(NH // 2):
                tb = TRANSPOSE_BANKS[(ND + n) % 2]
                dve.wait_ge(bank_empty[tb], (ND + n) // 2 + 1)
                for k in (2 * n, 2 * n + 1):
                    nc.vector.tensor_scalar(gW2T[:, k, :], W2T[:, k, :], gamma_c[:, k:k + 1], None, ALU.mult)\
                      .then_inc(W2T_scaled, 1)
            dve.wait_ge(bank_full[0], 1)
            nc.vector.tensor_copy(bW2_row[:, :], banks[0][:, 0:D]).then_inc(bank_empty[0], 1)
            build_H(0)

            def graph(b, more):
                dve.wait_ge(dn_ready, b * NT + NT)
                nc.vector.tensor_scalar(dn_pos, dn, 0.0, None, ALU.is_gt).then_inc(rDn_part, 1)
                nc.vector.tensor_scalar(dn_safe, dn, TINY, None, ALU.max).then_inc(rDn_part, 1)
                dve.wait_ge(rDn_part, b * 3 + 2)
                nc.vector.reciprocal(dn_inv, dn_safe).then_inc(rDn_part, 1)
                dve.wait_ge(rDn_part, b * 3 + 3)
                nc.vector.tensor_tensor(rDn, dn_inv, dn_pos, ALU.mult).then_inc(rDn_ready, 1)

                for e in range(NT):
                    dve.wait_ge(*full("S1", e, b))
                    nc.vector.tensor_scalar(be_safe[:, e:e + 1], bank("S1", e)[:, D:D + 1], 1.0, None, ALU.max)\
                      .then_inc(be_done, 1)
                    dve.wait_ge(be_done, b * NT + e + 1)
                    nc.vector.reciprocal(rBe[:, e:e + 1], be_safe[:, e:e + 1]).then_inc(rBe_ready, 1)
                    if e > 0:
                        build_HT(e - 1, b)
                    take_m_lo("S1", e, b, e)
                build_HT(NT - 1, b)

                dve.wait_ge(rDn_ready, b + 1)
                for s in range(NT + LAG_Q):
                    if s < NT:
                        dve.wait_ge(*full("P", s, b))
                        empties_bank(nc.vector.scalar_tensor_tensor(
                            out=hrow[:, s % H_SLOTS, :], in0=bank("P", s)[:, :], scalar=rDn[:, s:s + 1],
                            in1=b1_row[:, :], op0=ALU.mult, op1=ALU.add), "P", s)
                    if 0 <= s - 1 < NT:
                        normalise("h", 0, hrow[:, (s - 1) % H_SLOTS, :], std_h, rstd_h, s - 1, b)
                    if s < NT:
                        dve.wait_ge(relu_done, b * NT + s + 1)
                        moments("h", 0, hrow[:, s % H_SLOTS, :], s, b)
                    if s >= LAG_Q:
                        i = s - LAG_Q
                        dve.wait_ge(*full("Q", i, b))
                        if i >= 2:
                            dve.wait_ge(q_split, b * NT + i - 1)
                        empties_bank(nc.vector.tensor_tensor(q_f32[:, i % 2, :], bank("Q", i)[:, 0:D],
                                                             bW2_row[:, :], ALU.add), "Q", i)
                for e in range(NT):
                    take_m_lo("S3", e, b, NT + e)

                dve.wait_ge(xb_ready, b + 1)
                for i in range(NT + 1):
                    if i < NT:
                        dve.wait_ge(*full("S4", i, b))
                        empties_bank(nc.vector.scalar_tensor_tensor(
                            out=xres[:, i, :], in0=bank("S4", i)[:, 0:D], scalar=rDn[:, i:i + 1],
                            in1=xres[:, i, :], op0=ALU.mult, op1=ALU.add), "S4", i)
                        dve.wait_ge(*emptied("S4", i, b))
                        moments("1", 1, xres[:, i, :], i, b)
                    if i > 0:
                        normalise("1", 1, xres[:, i - 1, :], std_1, rstd_1, i - 1, b)
                nc.vector.memset(yv[:, :, 2 * D:YP], 1.0).then_inc(y_ones, 1)
                if more:
                    build_H(b + 1)
                for i in range(NT + 1):
                    if i < NT:
                        dve.wait_ge(*full("L", i, b))
                        nc.vector.tensor_scalar(deg_safe[:, i:i + 1], bank("L", i)[:, D:D + 1], DEG_EPS, None,
                                                ALU.max).then_inc(deg_done, 1)
                        dve.wait_ge(deg_done, b * NT + i + 1)
                        nc.vector.reciprocal(rdeg[:, i:i + 1], deg_safe[:, i:i + 1]).then_inc(rdeg_done, 1)
                        dve.wait_ge(rdeg_done, b * NT + i + 1)
                        empties_bank(nc.vector.scalar_tensor_tensor(
                            out=o_f32[:, i % 2, :], in0=bank("L", i)[:, 0:D], scalar=rdeg[:, i:i + 1],
                            in1=yv[:, i, 0:D], op0=ALU.mult, op1=ALU.add), "L", i)
                        dve.wait_ge(*emptied("L", i, b))
                        nc.vector.scalar_tensor_tensor(out=xres[:, i, :], in0=o_f32[:, i % 2, :], scalar=0.0,
                                                       in1=xres[:, i, :], op0=ALU.max, op1=ALU.add)\
                          .then_inc(sum_done, 1)
                        dve.wait_ge(sum_done, b * NT + i + 1)
                        moments("o", 2, xres[:, i, :], i, b)
                    if i > 0:
                        normalise("o", 2, xres[:, i - 1, :], std_o, rstd_o, i - 1, b)

            over_graphs(dve, graph)

        @block.tensor
        def _(pe):
            mm = nc.tensor.matmul

            pe.wait_ge(ident_ready, 1)
            pe.wait_ge(weights_loaded, 16 * 3)
            fours = [[W1n[:, h, d * P:(d + 1) * P] for h in range(NH)] for d in range(ND)] + \
                    [[W2n[:, o, k * P:(k + 1) * P] for k in (2 * n, 2 * n + 1) for o in range(ND)]
                     for n in range(NH // 2)] + \
                    [[WLn[:, o, (side * ND + d) * P:(side * ND + d + 1) * P] for side in range(2) for o in range(ND)]
                     for d in range(ND)]
            for n, four in enumerate(fours):
                tb = TRANSPOSE_BANKS[n % 2]
                if n >= 2:
                    pe.wait_ge(bank_empty[tb], n // 2)
                for j, src in enumerate(four):
                    last = nc.tensor.transpose(banks[tb][:, j * P:(j + 1) * P], src, ident[:, :])
                last.then_inc(bank_full[tb], 1)
            pe.wait_ge(beta_wide_done, NH)
            for n in range(NH // 2):
                pe.wait_ge(bank_empty[TRANSPOSE_BANKS[(ND + n) % 2]], (ND + n) // 2 + 1)
            for k in range(NH):
                last = mm(banks[0][:, 0:D], beta_wide[:, k, :], W2T[:, k, :], start=(k == 0), stop=(k == NH - 1))
            last.then_inc(bank_full[0], 1)
            pe.wait_ge(W2T_scaled, NH)
            pe.wait_ge(ones_ready, 1)

            def tiled(stage, b, n_cols, ready, parts, operands):
                def one(i, k):
                    for part in range(parts):
                        lhsT, rhs = operands(k, i, part)
                        last = mm(bank(stage, i)[:, 0:n_cols], lhsT, rhs, start=(k == 0 and part == 0),
                                  stop=(k == NT - 1 and part == parts - 1))
                    if k == NT - 1:
                        fills_bank(last, stage, i)

                for k in range(NT):
                    ready(k)
                    for i in range(GROUP):
                        if k == 0:
                            pe.wait_ge(*free(stage, i, b))
                        one(i, k)
                for i in range(GROUP, NT):
                    pe.wait_ge(*free(stage, i, b))
                    for k in range(NT):
                        one(i, k)

            def graph(b, more):
                pe.wait_ge(x_split, b + 1)
                for e in range(NT):
                    pe.wait_ge(*free("S1", e, b))
                    acc = bank("S1", e)
                    for c in range(NT):
                        if e == 0:
                            pe.wait_ge(H_ready, b * NT + c + 1)
                        lhsT = H[:, c, e * P:(e + 1) * P]
                        hi = (acc[:, 0:DP], lhsT, x_hi[:, c, :])
                        lo = (acc[:, 0:D], lhsT, x_lo[:, c, :])
                        for n, args in enumerate((hi, lo) if c < NT - 1 else (lo, hi)):
                            last = mm(*args, start=(c == 0 and n == 0), stop=(c == NT - 1 and n == 1))
                    fills_bank(last, "S1", e)
                    for half in range(2):
                        job = 2 * e + half
                        pe.wait_ge(*free("TA", job, b))
                        for k in range(4):
                            kt = half * 4 + k
                            last = nc.tensor.transpose(bank("TA", job)[:, k * P:(k + 1) * P],
                                                       raw[:, e, kt * P:(kt + 1) * P], ident[:, :])
                        fills_bank(last, "TA", job)

                for ch in range(NCH):
                    pe.wait_ge(HT_ready, b * NT + (ch + 1) * (NT // NCH))
                    for k in range(NT):
                        if ch == 0:
                            pe.wait_ge(*emptied("S1", k, b))
                        for d in range(ND):
                            job = ch * ND + d
                            if k == 0:
                                pe.wait_ge(*free("S2", job, b))
                            for n, m in enumerate((m_hi, m_lo)):
                                last = mm(bank("S2", job)[:, :], m[:, k, d * P:(d + 1) * P],
                                          HT[:, k, ch * CH:(ch + 1) * CH], start=(k == 0 and n == 0),
                                          stop=(k == NT - 1 and n == 1))
                            if k == NT - 1:
                                fills_bank(last, "S2", job)

                for s in range(NT + LAG_Q):
                    if s < NT:
                        pe.wait_ge(*free("P", s, b))
                        if s % (CH // P) == 0:
                            for d in range(ND):
                                pe.wait_ge(*emptied("S2", s // (CH // P) * ND + d, b))
                        for d in range(ND):
                            last = mm(bank("P", s)[:, :], zT[:, d, s * P:(s + 1) * P], W1T[:, d, :],
                                      start=(d == 0), stop=(d == ND - 1))
                        fills_bank(last, "P", s)
                    i = s - LAG_T
                    if 0 <= i < NT:
                        pe.wait_ge(*free("TH", i, b))
                        pe.wait_ge(normed["h"], b * NT + i + 1)
                        for k in range(NH):
                            last = nc.tensor.transpose(bank("TH", i)[:, k * P:(k + 1) * P],
                                                       hrow[:, i % H_SLOTS, k * P:(k + 1) * P], ident[:, :])
                        fills_bank(last, "TH", i)
                    i = s - LAG_Q
                    if 0 <= i < NT:
                        pe.wait_ge(*free("Q", i, b))
                        pe.wait_ge(*emptied("TH", i, b))
                        for k in range(NH):
                            last = mm(bank("Q", i)[:, 0:D], xnT[:, i % 2, k, :], gW2T[:, k, :],
                                      start=(k == 0), stop=(k == NH - 1))
                        fills_bank(last, "Q", i)

                tiled("S3", b, D, lambda c: pe.wait_ge(q_split, b * NT + c + 1), 2,
                      lambda c, e, part: (H[:, c, e * P:(e + 1) * P], (x_hi, x_lo)[part][:, c, 0:D]))
                tiled("S4", b, D, lambda e: pe.wait_ge(*emptied("S3", e, b)), 2,
                      lambda e, i, part: (HT[:, e, i * P:(i + 1) * P], (m_hi, m_lo)[part][:, e, :]))

                for i in range(NT + 1):
                    if i < NT:
                        pe.wait_ge(*free("TX", i, b))
                        pe.wait_ge(normed["1"], b * NT + i + 1)
                        for d in range(ND):
                            last = nc.tensor.transpose(bank("TX", i)[:, d * P:(d + 1) * P],
                                                       xres[:, i, d * P:(d + 1) * P], ident[:, :])
                        fills_bank(last, "TX", i)
                    if i > 0:
                        j = i - 1
                        pe.wait_ge(*free("V", j, b))
                        pe.wait_ge(*emptied("TX", j, b))
                        for d in range(ND):
                            last = mm(bank("V", j)[:, :], x1T[:, j % 2, d, :], WLT[:, d, :],
                                      start=(d == 0), stop=(d == ND - 1))
                        fills_bank(last, "V", j)

                pe.wait_ge(y_ones, b + 1)
                tiled("L", b, D + 1, lambda j: pe.wait_ge(*emptied("V", j, b)), 1,
                      lambda j, i, part: (adjT[:, j, i * P:(i + 1) * P], yv[:, j, D:YP]))

            over_graphs(pe, graph)


_INS = ['x', 'adj', 'L0_gnn_W1', 'L0_gnn_b1', 'L0_gnn_gamma', 'L0_gnn_beta', 'L0_gnn_W2', 'L0_gnn_b2', 'L1_gnn_W']


def kernel(**inputs):
    import numpy as _np
    import concourse.bacc as _bacc
    from concourse import mybir as _mybir
    from concourse.bass_utils import run_bass_kernel_spmd as _run

    nc = _bacc.Bacc("TRN2", target_bir_lowering=False, num_devices=1)
    arrays, args = {}, []
    for name in _INS:
        a = _np.ascontiguousarray(inputs[name])
        arrays[f"in_{name}_dram"] = a
        args.append(nc.dram_tensor(f"in_{name}_dram", a.shape, _mybir.dt.from_np(a.dtype), kind="ExternalInput").ap())
    shape = inputs['x'].shape
    args.append(nc.dram_tensor("out_0_dram", shape, _mybir.dt.from_np(_np.dtype('float32')),
                               kind="ExternalOutput").ap())
    graph_net(nc, *args)
    r = _run(nc, [arrays], core_ids=[0])
    return r.results[0]["out_0_dram"]
```

```python
from contextlib import ExitStack

import concourse.bass as bass
from concourse import mybir

F32 = mybir.dt.float32
F32R = mybir.dt.float32r
BF16 = mybir.dt.bfloat16
ALU = mybir.AluOpType
ACT = mybir.ActivationFunctionType

P = 128
NORM_EPS = 1e-5
DEG_EPS = 1e-6
TINY = 1.1754944e-38

PRODUCT_BANKS = {
    "S1": (0, 1, 2, 3, 4, 5, 0, 1),
    "S2": (2, 3, 4, 5),
    "P": (0, 1, 2, 0, 1, 2, 0, 1),
    "Q": (3, 4, 5, 3, 4, 5, 3, 4),
    "S3": (0, 1, 2, 5, 3, 4, 0, 1),
    "S4": (2, 5, 3, 4, 0, 1, 2, 5),
    "V": (3, 4, 0, 1, 3, 4, 0, 1),
    "L": (2, 5, 3, 4, 0, 1, 4, 5),
}
TRANSPOSE_BANKS = (6, 7)
N_BANKS = 8
GROUP = 2
SECOND_CHUNK = {0: (0, 1, 2), 1: (3, 4), 2: (5, 6), 3: (7,)}
LAG_T = 3
LAG_Q = 4
H_SLOTS = 4


def graph_net(nc, x, adj, W1, b1, gamma, beta, W2, b2, WL, out):
    B, C, D = x.shape
    DH = W1.shape[0]
    NT = C // P
    ND = D // P
    NH = DH // P
    CH = 512
    NCH = C // CH
    assert NCH == 2 and NT == 8
    DP = D + 2
    YP = 2 * D + 1

    setup_fills = [1, 0, 0, 0, 0, 0, 3, 3]
    setup_empties = [1, 1, 1, 1, 1, 1, 3, 3]
    bank_of, nth = {}, {}
    fills = [0] * N_BANKS
    turn = [0]

    def add_job(stage, tile):
        if stage in PRODUCT_BANKS:
            bank = PRODUCT_BANKS[stage][tile]
        else:
            bank = TRANSPOSE_BANKS[turn[0] % 2]
            turn[0] += 1
        bank_of[stage, tile] = bank
        nth[stage, tile] = fills[bank]
        fills[bank] += 1

    for e in range(NT):
        add_job("S1", e)
        add_job("TA", 2 * e)
        add_job("TA", 2 * e + 1)
    for j in range(NCH * ND):
        add_job("S2", j)
    for s in range(NT + LAG_Q):
        if s < NT:
            add_job("P", s)
        if 0 <= s - LAG_T < NT:
            add_job("TH", s - LAG_T)
        if 0 <= s - LAG_Q < NT:
            add_job("Q", s - LAG_Q)
    for stage in ("S3", "S4"):
        for e in range(NT):
            add_job(stage, e)
    for i in range(NT + 1):
        if i < NT:
            add_job("TX", i)
        if i > 0:
            add_job("V", i - 1)
    for i in range(NT):
        add_job("L", i)

    ctx = ExitStack()
    with ctx:
        at = [(nc.sbuf_base + 63) // 64 * 64]

        def place(name, shape, dt, offset=None):
            n = 4 if dt != BF16 else 2
            for d in shape[1:]:
                n *= d
            if offset is None:
                offset = at[0]
                at[0] += (n + 63) // 64 * 64
            return nc.alloc_sbuf_tensor_at(name, shape, dt, offset=offset), offset, offset + (n + 63) // 64 * 64

        raw, raw_at, _ = place("raw", [P, NT, C], F32)
        H, _, _ = place("H", [P, NT, C], F32R)
        adjT, adjT_at, _ = place("adjT", [P, NT, C], F32)
        HT, HT_at, _ = place("HT", [P, NT, C], F32R)
        x_hi, _, _ = place("x_hi", [P, NT, DP], F32R)
        x_lo, _, _ = place("x_lo", [P, NT, D], F32R)
        m_hi, _, _ = place("m_hi", [P, NT, D], F32R)
        m_lo, _, _ = place("m_lo", [P, NT, D], F32R)
        x_in, _, _ = place("x_in", [P, NT, D], F32)
        xres, _, _ = place("xres", [P, NT, D], F32)
        w_row, _, _ = place("w_row", [P, C], F32)
        W1T, _, _ = place("W1T", [P, ND, DH], F32)
        gW2T, _, _ = place("gW2T", [P, NH, D], F32)
        WLT, _, _ = place("WLT", [P, ND, 2 * D], F32)
        b1_row, _, _ = place("b1_row", [P, DH], F32)
        b2_row, _, _ = place("b2_row", [P, D], F32)
        bW2_row, _, _ = place("bW2_row", [P, D], F32)
        x1T, _, _ = place("x1T", [P, 2, ND, P], F32)
        q_f32, q_at, _ = place("q_f32", [P, 2, D], F32)
        o_f32, _, _ = place("o_f32", [P, 2, D], F32)
        ident, _, _ = place("ident", [P, P], F32)
        small, _, _ = place("small", [P, 20, NT], F32)
        zT, _, nxt = place("zT", [P, ND, C], F32, raw_at)
        hrow, _, nxt = place("hrow", [P, H_SLOTS, DH], F32, nxt)
        xnT, _, _ = place("xnT", [P, 2, NH, P], F32, nxt)
        yv, _, _ = place("yv", [P, NT, YP], F32, HT_at)
        unread, _, _ = place("unread", [P, C], F32, q_at)
        W1n, _, nxt = place("W1n", [P, NH, D], F32, adjT_at)
        W2n, _, nxt = place("W2n", [P, ND, DH], F32, nxt)
        WLn, _, nxt = place("WLn", [P, ND, 2 * D], F32, nxt)
        W2T, _, nxt = place("W2T", [P, NH, D], F32, nxt)
        beta_wide, _, _ = place("beta_wide", [P, NH, P], F32, nxt)

        def col(n):
            return small[:, n, :]

        (dn, dn_pos, dn_safe, dn_inv, rDn, be_safe, rBe, deg_safe, rdeg, std_h, rstd_h, std_1, rstd_1,
         std_o, rstd_o, gb) = (col(n) for n in range(16))
        gamma_c, beta_c, eps_c = gb[:, 0:NH], gb[:, NH:2 * NH], small[:, 16, 0:1]
        stats, _, _ = place("stats", [P, 3, NT, 6], F32)
        mv, _, _ = place("mv", [P, 3, NT, 2], F32)
        assert NT >= 2 * NH and at[0] <= nc.sbuf_usable_end, (at[0], nc.sbuf_usable_end)

        banks = [ctx.enter_context(nc.psum_tensor(f"bank{n}", [P, 512], F32)) for n in range(N_BANKS)]

        def sem(name):
            return ctx.enter_context(nc.semaphore(name))

        bank_full = [sem(f"bank_full{n}") for n in range(N_BANKS)]
        bank_empty = [sem(f"bank_empty{n}") for n in range(N_BANKS)]
        raw_loaded = [sem(f"raw_loaded{n}") for n in range(NT // 2)]
        x_loaded, w_loaded, weights_loaded, rows_loaded, bias_loaded, table_loaded = (
            sem(n) for n in ("x_loaded", "w_loaded", "weights_loaded", "rows_loaded", "bias_loaded",
                              "table_loaded"))
        ident_zero, ident_ready, eps_ready, ones_ready, x_split, x_hi_done, xb_part, xb_ready = (
            sem(n) for n in ("ident_zero", "ident_ready", "eps_ready", "ones_ready", "x_split", "x_hi_done",
                             "xb_part", "xb_ready"))
        q_hi_done, q_split, y_ones = (sem(n) for n in ("q_hi_done", "q_split", "y_ones"))
        H_ready, HT_ready, dn_ready, rDn_part, rDn_ready = (
            sem(n) for n in ("H_ready", "HT_ready", "dn_ready", "rDn_part", "rDn_ready"))
        be_done, rBe_ready, m_hi_done = (sem(n) for n in ("be_done", "rBe_ready", "m_hi_done"))
        relu_done = sem("relu_done")
        deg_done, rdeg_done, o_done, sum_done = (sem(n) for n in ("deg_done", "rdeg_done", "o_done", "sum_done"))
        norms = ("h", "1", "o")
        stats_done = sem("stats_done")
        var_done = {n: sem(f"var_done_{n}") for n in norms}
        std_done = {n: sem(f"std_done_{n}") for n in norms}
        rstd_done = {n: sem(f"rstd_done_{n}") for n in norms}
        normed = {n: sem(f"normed_{n}") for n in norms}
        W2T_scaled, beta_wide_done = sem("W2T_scaled"), sem("beta_wide_done")
        out_stored = sem("out_stored")

        def bank(stage, tile):
            return banks[bank_of[stage, tile]]

        def full(stage, tile, b):
            n = bank_of[stage, tile]
            return bank_full[n], b * fills[n] + (setup_fills[n] + nth[stage, tile] + 1)

        def emptied(stage, tile, b):
            n = bank_of[stage, tile]
            return bank_empty[n], b * fills[n] + (setup_empties[n] + nth[stage, tile] + 1)

        def free(stage, tile, b):
            n = bank_of[stage, tile]
            return bank_empty[n], b * fills[n] + (setup_empties[n] + nth[stage, tile])

        def fills_bank(ins, stage, tile):
            ins.then_inc(bank_full[bank_of[stage, tile]], 1)

        def empties_bank(ins, stage, tile):
            ins.then_inc(bank_empty[bank_of[stage, tile]], 1)

        def over_graphs(eng, graph):
            with eng.Fori(0, B - 1) as b:
                graph(b, True)
            graph(B - 1, False)

        block = ctx.enter_context(nc.Block())

        @block.sync
        def _(sp):
            def load_graph(b):
                for j in range(NT // 2):
                    sp.dma_start(raw[:, 2 * j:2 * j + 2, :],
                                 adj[b, 2 * j * P:(2 * j + 2) * P, :].rearrange("(t p) e -> p t e", p=P))\
                      .then_inc(raw_loaded[j], 16)

            def load_x(b):
                sp.dma_start(x_in[:, :, :], x[b, :, :].rearrange("(t p) d -> p t d", p=P)).then_inc(x_loaded, 16)

            def load_w(b):
                sp.dma_start(w_row[:, :], adj[b, 0, :].partition_broadcast(P)).then_inc(w_loaded, 16)

            sp.dma_start(gamma_c, gamma.rearrange("(k p) -> p k", p=P), allow_slow_non_contiguous=True)\
              .then_inc(rows_loaded, 16)
            sp.dma_start(beta_c, beta.rearrange("(k p) -> p k", p=P), allow_slow_non_contiguous=True)\
              .then_inc(rows_loaded, 16)
            sp.dma_start(W1n[:, :, :], W1.rearrange("(t p) d -> p t d", p=P)).then_inc(weights_loaded, 16)
            sp.dma_start(W2n[:, :, :], W2.rearrange("(t p) d -> p t d", p=P)).then_inc(weights_loaded, 16)
            sp.dma_start(WLn[:, :, :], WL.rearrange("(t p) d -> p t d", p=P)).then_inc(weights_loaded, 16)
            load_x(0)
            load_graph(0)
            load_w(0)
            sp.dma_start(b1_row[:, :], b1.partition_broadcast(P)).then_inc(bias_loaded, 16)
            sp.dma_start(b2_row[:, :], b2.partition_broadcast(P)).then_inc(bias_loaded, 16)

            def graph(b, more):
                if more:
                    sp.wait_ge(dn_ready, b * NT + NT)
                    load_w(b + 1)
                    sp.wait_ge(xb_ready, b + 1)
                    sp.wait_ge(x_split, b + 1)
                    load_x(b + 1)
                    sp.wait_ge(*full("Q", NT - 1, b))
                    load_graph(b + 1)
                for j in range(NT // 2):
                    sp.wait_ge(normed["o"], b * NT + 2 * j + 2)
                    sp.dma_start(out[b, 2 * j * P:(2 * j + 2) * P, :].rearrange("(t p) d -> p t d", p=P),
                                 xres[:, 2 * j:2 * j + 2, :]).then_inc(out_stored, 16)

            over_graphs(sp, graph)
            sp.wait_ge(out_stored, 16 * (NT // 2) * B)

        @block.gpsimd
        def _(pool):
            nc.gpsimd.memset(ident[:, :], 0.0).then_inc(ident_zero, 1)
            nc.gpsimd.memset(x_hi[:, :, D:DP].bitcast(F32), 1.0).then_inc(ones_ready, 1)
            nc.gpsimd.memset(eps_c, NORM_EPS).then_inc(eps_ready, 1)
            pool.wait_ge(ident_zero, 1)
            nc.gpsimd.affine_select(out=ident[:, :], in_=ident[:, :], compare_op=ALU.not_equal, fill=1.0,
                                    base=0, pattern=[[-1, P]], channel_multiplier=1).then_inc(ident_ready, 1)

            def split_x(b):
                pool.wait_ge(x_hi_done, b + 1)
                nc.gpsimd.tensor_tensor(x_lo[:, :, :], x_in[:, :, :], x_hi[:, :, 0:D].bitcast(F32), ALU.subtract)\
                  .then_inc(x_split, 1)

            split_x(0)
            pool.wait_ge(bias_loaded, 16 * 2)

            def residual(b):
                nc.gpsimd.tensor_tensor(xres[:, :, :], x_in[:, :, :], x_in[:, :, :], ALU.add).then_inc(xb_part, 1)
                pool.wait_ge(xb_part, b + 1)
                nc.gpsimd.tensor_tensor(xres[:, :, :], xres[:, :, :],
                                        b2_row[:, :].unsqueeze(1).to_broadcast([P, NT, D]), ALU.add)\
                  .then_inc(xb_ready, 1)

            residual(0)

            def graph(b, more):
                for i in range(NT):
                    pool.wait_ge(q_hi_done, b * NT + i + 1)
                    nc.gpsimd.tensor_tensor(x_lo[:, i, :], q_f32[:, i % 2, :], x_hi[:, i, 0:D].bitcast(F32),
                                            ALU.subtract).then_inc(q_split, 1)
                if more:
                    split_x(b + 1)
                    pool.wait_ge(out_stored, b * (16 * (NT // 2)) + 16 * (NT // 2))
                    residual(b + 1)

            over_graphs(pool, graph)

        @block.scalar
        def _(act):
            act.wait_ge(eps_ready, 1)
            nc.scalar.activation(small[:, 17, 0:1], eps_c, ACT.Sqrt).then_inc(table_loaded, 1)
            targets = [W1T[:, d, :] for d in range(ND)] + \
                      [W2T[:, 2 * k:2 * k + 2, :].rearrange("p k o -> p (k o)") for k in range(NH // 2)] + \
                      [WLT[:, d, :] for d in range(ND)]
            for n, target in enumerate(targets):
                tb = TRANSPOSE_BANKS[n % 2]
                act.wait_ge(bank_full[tb], n // 2 + 1)
                nc.scalar.activation(target, banks[tb][:, :], ACT.Copy).then_inc(bank_empty[tb], 1)

            def take_m_hi(stage, e, b, n):
                act.wait_ge(*full(stage, e, b))
                act.wait_ge(rBe_ready, b * NT + (e + 1 if stage == "S1" else NT))
                nc.scalar.activation(m_hi[:, e, :], bank(stage, e)[:, 0:D], ACT.Identity, scale=rBe[:, e:e + 1])\
                  .then_inc(m_hi_done, 1)

            def root(norm, which, std, i, b):
                act.wait_ge(var_done[norm], b * NT + i + 1)
                nc.scalar.activation(std[:, i:i + 1], mv[:, which, i, 1:2], ACT.Sqrt, bias=eps_c)\
                  .then_inc(std_done[norm], 1)

            def split_x_hi(b):
                act.wait_ge(x_loaded, b * 16 + 16)
                nc.scalar.activation(x_hi[:, :, 0:D], x_in[:, :, :], ACT.Copy).then_inc(x_hi_done, 1)

            split_x_hi(0)

            def graph(b, more):
                for e in range(NT):
                    for half in range(2):
                        job = 2 * e + half
                        act.wait_ge(*full("TA", job, b))
                        empties_bank(nc.scalar.activation(
                            adjT[:, half * 4:half * 4 + 4, e * P:(e + 1) * P],
                            bank("TA", job)[:, :].rearrange("p (k c) -> p k c", c=P), ACT.Copy), "TA", job)
                    take_m_hi("S1", e, b, e)
                def take_zT(ch):
                    for d in range(ND):
                        act.wait_ge(*full("S2", ch * ND + d, b))
                        act.wait_ge(dn_ready, b * NT + ND)
                        empties_bank(nc.scalar.activation(zT[:, d, ch * CH:(ch + 1) * CH],
                                                          bank("S2", ch * ND + d)[:, :], ACT.Copy), "S2", ch * ND + d)

                take_zT(0)
                for s in range(NT + LAG_Q):
                    if s < NT:
                        act.wait_ge(*emptied("P", s, b))
                        nc.scalar.activation(hrow[:, s % H_SLOTS, :], hrow[:, s % H_SLOTS, :], ACT.Relu)\
                          .then_inc(relu_done, 1)
                    if s == max(SECOND_CHUNK) - 1:
                        take_zT(1)
                    if 0 <= s - LAG_T < NT:
                        i = s - LAG_T
                        act.wait_ge(*full("TH", i, b))
                        empties_bank(nc.scalar.activation(xnT[:, i % 2, :, :].rearrange("p k c -> p (k c)"),
                                                          bank("TH", i)[:, :], ACT.Copy), "TH", i)
                    if s < NT:
                        root("h", 0, std_h, s, b)
                    if s >= LAG_Q:
                        i = s - LAG_Q
                        act.wait_ge(*emptied("Q", i, b))
                        nc.scalar.activation(x_hi[:, i, 0:D], q_f32[:, i % 2, :], ACT.Copy).then_inc(q_hi_done, 1)
                for e in range(NT):
                    take_m_hi("S3", e, b, NT + e)
                if more:
                    split_x_hi(b + 1)
                def take_x1T(i):
                    act.wait_ge(*full("TX", i, b))
                    empties_bank(nc.scalar.activation(x1T[:, i % 2, :, :].rearrange("p k c -> p (k c)"),
                                                      bank("TX", i)[:, 0:D], ACT.Copy), "TX", i)

                for i in range(NT - 2):
                    root("1", 1, std_1, i, b)
                take_x1T(0)
                take_x1T(1)
                root("1", 1, std_1, NT - 2, b)
                root("1", 1, std_1, NT - 1, b)
                for i in range(NT):
                    act.wait_ge(*full("V", i, b))
                    empties_bank(nc.scalar.activation(yv[:, i, 0:2 * D], bank("V", i)[:, :], ACT.Copy), "V", i)
                    if i + 2 < NT:
                        take_x1T(i + 2)
                for i in range(NT):
                    root("o", 2, std_o, i, b)

            over_graphs(act, graph)

        @block.vector
        def _(dve):
            def build_H(b):
                for c in range(NT):
                    dve.wait_ge(raw_loaded[c // 2], b * 16 + 16)
                    nc.vector.tensor_scalar(H[:, c, :], raw[:, c, :], 0.0, None, ALU.not_equal).then_inc(H_ready, 1)

            def build_rDn(b):
                dve.wait_ge(w_loaded, b * 16 + 16)
                for c in range(NT):
                    if c > 0:
                        dve.wait_ge(dn_ready, b * NT + c)
                    nc.vector.scalar_tensor_tensor(out=unread[:, :], in0=raw[:, c, :], scalar=0.0, in1=w_row[:, :],
                                                   op0=ALU.not_equal, op1=ALU.mult,
                                                   accum_out=dn[:, c:c + 1]).then_inc(dn_ready, 1)
                dve.wait_ge(dn_ready, b * NT + NT)
                nc.vector.tensor_scalar(dn_pos, dn, 0.0, None, ALU.is_gt).then_inc(rDn_part, 1)
                nc.vector.tensor_scalar(dn_safe, dn, TINY, None, ALU.max).then_inc(rDn_part, 1)
                dve.wait_ge(rDn_part, b * 3 + 2)
                nc.vector.reciprocal(dn_inv, dn_safe).then_inc(rDn_part, 1)
                dve.wait_ge(rDn_part, b * 3 + 3)
                nc.vector.tensor_tensor(rDn, dn_inv, dn_pos, ALU.mult).then_inc(rDn_ready, 1)

            def inverse_root(norm, std, rstd, i, b):
                dve.wait_ge(std_done[norm], b * NT + i + 1)
                nc.vector.reciprocal(rstd[:, i:i + 1], std[:, i:i + 1]).then_inc(rstd_done[norm], 1)

            def centre(norm, which, rows, rstd, i, b):
                dve.wait_ge(rstd_done[norm], b * NT + i + 1)
                nc.vector.tensor_scalar(rows, rows, mv[:, which, i, 0:1], rstd[:, i:i + 1],
                                        ALU.subtract, ALU.mult).then_inc(normed[norm], 1)

            def moments(norm, which, src, i, b):
                nc.vector.bn_stats(stats[:, which, i, :], src)
                dve.drain()
                nc.vector.bn_aggr(mv[:, which, i, :], stats[:, which, i, :]).then_inc(var_done[norm], 1)

            def take_m_lo(stage, e, b, n):
                dve.wait_ge(m_hi_done, b * (2 * NT) + (n + 1))
                empties_bank(nc.vector.scalar_tensor_tensor(
                    out=m_lo[:, e, :], in0=bank(stage, e)[:, 0:D], scalar=rBe[:, e:e + 1],
                    in1=m_hi[:, e, :].bitcast(F32), op0=ALU.mult, op1=ALU.subtract), stage, e)

            def build_HT(c, b):
                dve.wait_ge(*emptied("TA", 2 * c, b))
                dve.wait_ge(*emptied("TA", 2 * c + 1, b))
                nc.vector.tensor_scalar(HT[:, :, c * P:(c + 1) * P], adjT[:, :, c * P:(c + 1) * P], 0.0, None,
                                        ALU.not_equal).then_inc(HT_ready, 1)

            for n in range(1, TRANSPOSE_BANKS[0]):
                nc.vector.memset(banks[n][:, 0:1], 0.0).then_inc(bank_empty[n], 1)
            dve.wait_ge(rows_loaded, 16 * 2)
            for k in range(NH):
                nc.vector.tensor_copy(beta_wide[:, k, :], beta_c[:, k:k + 1].to_broadcast([P, P]))\
                  .then_inc(beta_wide_done, 1)
            for n in range(NH // 2):
                tb = TRANSPOSE_BANKS[(ND + n) % 2]
                dve.wait_ge(bank_empty[tb], (ND + n) // 2 + 1)
                for k in (2 * n, 2 * n + 1):
                    nc.vector.tensor_scalar(gW2T[:, k, :], W2T[:, k, :], gamma_c[:, k:k + 1], None, ALU.mult)\
                      .then_inc(W2T_scaled, 1)
            dve.wait_ge(bank_full[0], 1)
            nc.vector.tensor_copy(bW2_row[:, :], banks[0][:, 0:D]).then_inc(bank_empty[0], 1)
            build_H(0)

            def graph(b, more):
                for e in range(NT):
                    dve.wait_ge(*full("S1", e, b))
                    nc.vector.tensor_scalar(be_safe[:, e:e + 1], bank("S1", e)[:, D:D + 1], 1.0, None, ALU.max)\
                      .then_inc(be_done, 1)
                    dve.wait_ge(be_done, b * NT + e + 1)
                    nc.vector.reciprocal(rBe[:, e:e + 1], be_safe[:, e:e + 1]).then_inc(rBe_ready, 1)
                    if e > 0:
                        build_HT(e - 1, b)
                    take_m_lo("S1", e, b, e)
                build_HT(NT - 1, b)

                build_rDn(b)
                dve.wait_ge(bias_loaded, 16 * 2)
                dve.wait_ge(rDn_ready, b + 1)
                for s in range(NT + LAG_Q):
                    if s < NT:
                        dve.wait_ge(*full("P", s, b))
                        empties_bank(nc.vector.scalar_tensor_tensor(
                            out=hrow[:, s % H_SLOTS, :], in0=bank("P", s)[:, :], scalar=rDn[:, s:s + 1],
                            in1=b1_row[:, :], op0=ALU.mult, op1=ALU.add), "P", s)
                    if 0 <= s - 1 < NT:
                        inverse_root("h", std_h, rstd_h, s - 1, b)
                        centre("h", 0, hrow[:, (s - 1) % H_SLOTS, :], rstd_h, s - 1, b)
                    if s < NT:
                        dve.wait_ge(relu_done, b * NT + s + 1)
                        moments("h", 0, hrow[:, s % H_SLOTS, :], s, b)
                    if s >= LAG_Q:
                        i = s - LAG_Q
                        dve.wait_ge(*full("Q", i, b))
                        if i >= 2:
                            dve.wait_ge(q_split, b * NT + i - 1)
                        empties_bank(nc.vector.tensor_tensor(q_f32[:, i % 2, :], bank("Q", i)[:, 0:D],
                                                             bW2_row[:, :], ALU.add), "Q", i)
                for e in range(NT):
                    take_m_lo("S3", e, b, NT + e)

                dve.wait_ge(xb_ready, b + 1)
                for i in range(NT + 1):
                    if i < NT:
                        dve.wait_ge(*full("S4", i, b))
                        empties_bank(nc.vector.scalar_tensor_tensor(
                            out=xres[:, i, :], in0=bank("S4", i)[:, 0:D], scalar=rDn[:, i:i + 1],
                            in1=xres[:, i, :], op0=ALU.mult, op1=ALU.add), "S4", i)
                    if i > 0:
                        inverse_root("1", std_1, rstd_1, i - 1, b)
                    if i < NT:
                        dve.wait_ge(*emptied("S4", i, b))
                        nc.vector.bn_stats(stats[:, 1, i, :], xres[:, i, :]).then_inc(stats_done, 1)
                    if i > 0:
                        if i < NT:
                            dve.wait_ge(stats_done, b * NT + i + 1)
                        centre("1", 1, xres[:, i - 1, :], rstd_1, i - 1, b)
                    if i < NT:
                        if i == 0:
                            dve.drain()
                        nc.vector.bn_aggr(mv[:, 1, i, :], stats[:, 1, i, :]).then_inc(var_done["1"], 1)
                nc.vector.memset(yv[:, :, 2 * D:YP], 1.0).then_inc(y_ones, 1)
                if more:
                    build_H(b + 1)
                for i in range(NT + 1):
                    if i < NT:
                        dve.wait_ge(*full("L", i, b))
                        nc.vector.tensor_scalar(deg_safe[:, i:i + 1], bank("L", i)[:, D:D + 1], DEG_EPS, None,
                                                ALU.max).then_inc(deg_done, 1)
                    if i > 0:
                        inverse_root("o", std_o, rstd_o, i - 1, b)
                    if i < NT:
                        dve.wait_ge(deg_done, b * NT + i + 1)
                        nc.vector.reciprocal(rdeg[:, i:i + 1], deg_safe[:, i:i + 1]).then_inc(rdeg_done, 1)
                    if i > 0:
                        centre("o", 2, xres[:, i - 1, :], rstd_o, i - 1, b)
                    if i < NT:
                        dve.wait_ge(rdeg_done, b * NT + i + 1)
                        empties_bank(nc.vector.scalar_tensor_tensor(
                            out=o_f32[:, i % 2, :], in0=bank("L", i)[:, 0:D], scalar=rdeg[:, i:i + 1],
                            in1=yv[:, i, 0:D], op0=ALU.mult, op1=ALU.add), "L", i)
                        dve.wait_ge(*emptied("L", i, b))
                        nc.vector.scalar_tensor_tensor(out=xres[:, i, :], in0=o_f32[:, i % 2, :], scalar=0.0,
                                                       in1=xres[:, i, :], op0=ALU.max, op1=ALU.add)\
                          .then_inc(sum_done, 1)
                        dve.wait_ge(sum_done, b * NT + i + 1)
                        moments("o", 2, xres[:, i, :], i, b)

            over_graphs(dve, graph)

        @block.tensor
        def _(pe):
            mm = nc.tensor.matmul

            pe.wait_ge(ident_ready, 1)
            pe.wait_ge(weights_loaded, 16 * 3)
            fours = [[W1n[:, h, d * P:(d + 1) * P] for h in range(NH)] for d in range(ND)] + \
                    [[W2n[:, o, k * P:(k + 1) * P] for k in (2 * n, 2 * n + 1) for o in range(ND)]
                     for n in range(NH // 2)] + \
                    [[WLn[:, o, (side * ND + d) * P:(side * ND + d + 1) * P] for side in range(2) for o in range(ND)]
                     for d in range(ND)]
            for n, four in enumerate(fours):
                tb = TRANSPOSE_BANKS[n % 2]
                if n >= 2:
                    pe.wait_ge(bank_empty[tb], n // 2)
                for j, src in enumerate(four):
                    last = nc.tensor.transpose(banks[tb][:, j * P:(j + 1) * P], src, ident[:, :])
                last.then_inc(bank_full[tb], 1)
            pe.wait_ge(beta_wide_done, NH)
            for n in range(NH // 2):
                pe.wait_ge(bank_empty[TRANSPOSE_BANKS[(ND + n) % 2]], (ND + n) // 2 + 1)
            for k in range(NH):
                last = mm(banks[0][:, 0:D], beta_wide[:, k, :], W2T[:, k, :], start=(k == 0), stop=(k == NH - 1))
            last.then_inc(bank_full[0], 1)
            pe.wait_ge(W2T_scaled, NH)
            pe.wait_ge(ones_ready, 1)

            def tiled(stage, b, n_cols, ready, parts, operands, before_last=None):
                def one(i, k):
                    for part in range(parts):
                        lhsT, rhs = operands(k, i, part)
                        last = mm(bank(stage, i)[:, 0:n_cols], lhsT, rhs, start=(k == 0 and part == 0),
                                  stop=(k == NT - 1 and part == parts - 1))
                    if k == NT - 1:
                        fills_bank(last, stage, i)

                for k in range(NT):
                    ready(k)
                    for i in range(GROUP):
                        if k == 0:
                            pe.wait_ge(*free(stage, i, b))
                        one(i, k)
                for i in range(GROUP, NT):
                    if i == NT - 1 and before_last:
                        before_last()
                    pe.wait_ge(*free(stage, i, b))
                    for k in range(NT):
                        one(i, k)

            def graph(b, more):
                pe.wait_ge(x_split, b + 1)
                for e in range(NT):
                    pe.wait_ge(*free("S1", e, b))
                    acc = bank("S1", e)
                    for c in range(NT):
                        if e == 0:
                            pe.wait_ge(H_ready, b * NT + c + 1)
                        lhsT = H[:, c, e * P:(e + 1) * P]
                        hi = (acc[:, 0:DP], lhsT, x_hi[:, c, :])
                        lo = (acc[:, 0:D], lhsT, x_lo[:, c, :])
                        for n, args in enumerate((hi, lo) if c < NT - 1 else (lo, hi)):
                            last = mm(*args, start=(c == 0 and n == 0), stop=(c == NT - 1 and n == 1))
                    fills_bank(last, "S1", e)
                    for half in range(2):
                        job = 2 * e + half
                        pe.wait_ge(*free("TA", job, b))
                        for k in range(4):
                            kt = half * 4 + k
                            last = nc.tensor.transpose(bank("TA", job)[:, k * P:(k + 1) * P],
                                                       raw[:, e, kt * P:(kt + 1) * P], ident[:, :])
                        fills_bank(last, "TA", job)

                def s2_step(ch, k):
                    for d in range(ND):
                        job = ch * ND + d
                        if k == 0:
                            pe.wait_ge(*free("S2", job, b))
                        for n, m in enumerate((m_hi, m_lo)):
                            last = mm(bank("S2", job)[:, :], m[:, k, d * P:(d + 1) * P],
                                      HT[:, k, ch * CH:(ch + 1) * CH], start=(k == 0 and n == 0),
                                      stop=(k == NT - 1 and n == 1))
                        if k == NT - 1:
                            fills_bank(last, "S2", job)

                pe.wait_ge(HT_ready, b * NT + NT // NCH)
                for k in range(NT):
                    pe.wait_ge(*emptied("S1", k, b))
                    s2_step(0, k)
                pe.wait_ge(HT_ready, b * NT + NT)
                for s in range(NT + LAG_Q):
                    for k in SECOND_CHUNK.get(s, ()):
                        s2_step(1, k)
                    if s < NT:
                        pe.wait_ge(*free("P", s, b))
                        if s % (CH // P) == 0:
                            for d in range(ND):
                                pe.wait_ge(*emptied("S2", s // (CH // P) * ND + d, b))
                        for d in range(ND):
                            last = mm(bank("P", s)[:, :], zT[:, d, s * P:(s + 1) * P], W1T[:, d, :],
                                      start=(d == 0), stop=(d == ND - 1))
                        fills_bank(last, "P", s)
                    i = s - LAG_T
                    if 0 <= i < NT:
                        pe.wait_ge(*free("TH", i, b))
                        pe.wait_ge(normed["h"], b * NT + i + 1)
                        for k in range(NH):
                            last = nc.tensor.transpose(bank("TH", i)[:, k * P:(k + 1) * P],
                                                       hrow[:, i % H_SLOTS, k * P:(k + 1) * P], ident[:, :])
                        fills_bank(last, "TH", i)
                    i = s - LAG_Q
                    if 0 <= i < NT:
                        pe.wait_ge(*free("Q", i, b))
                        pe.wait_ge(*emptied("TH", i, b))
                        for k in range(NH):
                            last = mm(bank("Q", i)[:, 0:D], xnT[:, i % 2, k, :], gW2T[:, k, :],
                                      start=(k == 0), stop=(k == NH - 1))
                        fills_bank(last, "Q", i)

                def transpose_x1(i):
                    pe.wait_ge(*free("TX", i, b))
                    pe.wait_ge(normed["1"], b * NT + i + 1)
                    for d in range(ND):
                        last = nc.tensor.transpose(bank("TX", i)[:, d * P:(d + 1) * P],
                                                   xres[:, i, d * P:(d + 1) * P], ident[:, :])
                    fills_bank(last, "TX", i)

                tiled("S3", b, D, lambda c: pe.wait_ge(q_split, b * NT + c + 1), 2,
                      lambda c, e, part: (H[:, c, e * P:(e + 1) * P], (x_hi, x_lo)[part][:, c, 0:D]))
                tiled("S4", b, D, lambda e: pe.wait_ge(*emptied("S3", e, b)), 2,
                      lambda e, i, part: (HT[:, e, i * P:(i + 1) * P], (m_hi, m_lo)[part][:, e, :]),
                      before_last=lambda: (transpose_x1(0), transpose_x1(1)))

                for i in range(NT):
                    pe.wait_ge(*free("V", i, b))
                    pe.wait_ge(*emptied("TX", i, b))
                    for d in range(ND):
                        last = mm(bank("V", i)[:, :], x1T[:, i % 2, d, :], WLT[:, d, :],
                                  start=(d == 0), stop=(d == ND - 1))
                    fills_bank(last, "V", i)
                    if i + 2 < NT:
                        transpose_x1(i + 2)

                pe.wait_ge(y_ones, b + 1)
                tiled("L", b, D + 1, lambda j: pe.wait_ge(*emptied("V", j, b)), 1,
                      lambda j, i, part: (adjT[:, j, i * P:(i + 1) * P], yv[:, j, D:YP]))

            over_graphs(pe, graph)


_INS = ['x', 'adj', 'L0_gnn_W1', 'L0_gnn_b1', 'L0_gnn_gamma', 'L0_gnn_beta', 'L0_gnn_W2', 'L0_gnn_b2', 'L1_gnn_W']


def kernel(**inputs):
    import numpy as _np
    import concourse.bacc as _bacc
    from concourse import mybir as _mybir
    from concourse.bass_utils import run_bass_kernel_spmd as _run

    nc = _bacc.Bacc("TRN2", target_bir_lowering=False, num_devices=1)
    arrays, args = {}, []
    for name in _INS:
        a = _np.ascontiguousarray(inputs[name])
        arrays[f"in_{name}_dram"] = a
        args.append(nc.dram_tensor(f"in_{name}_dram", a.shape, _mybir.dt.from_np(a.dtype), kind="ExternalInput").ap())
    shape = inputs['x'].shape
    args.append(nc.dram_tensor("out_0_dram", shape, _mybir.dt.from_np(_np.dtype('float32')),
                               kind="ExternalOutput").ap())
    graph_net(nc, *args)
    r = _run(nc, [arrays], core_ids=[0])
    return r.results[0]["out_0_dram"]
```

```python
from contextlib import ExitStack

import concourse.bass as bass
from concourse import mybir

F32 = mybir.dt.float32
F32R = mybir.dt.float32r
BF16 = mybir.dt.bfloat16
ALU = mybir.AluOpType
ACT = mybir.ActivationFunctionType

P = 128
NORM_EPS = 1e-5
DEG_EPS = 1e-6
TINY = 1.1754944e-38

PRODUCT_BANKS = {
    "S1": (0, 1, 2, 3, 4, 5, 0, 1),
    "S2": (2, 3, 4, 5),
    "P": (0, 1, 2, 0, 1, 2, 0, 1),
    "Q": (3, 4, 5, 3, 4, 5, 3, 4),
    "S3": (0, 1, 2, 5, 3, 4, 0, 1),
    "S4": (2, 5, 3, 4, 0, 1, 2, 5),
    "V": (3, 4, 0, 1, 3, 4, 0, 1),
    "L": (2, 5, 3, 4, 0, 1, 4, 5),
}
TRANSPOSE_BANKS = (6, 7)
N_BANKS = 8
GROUP = 2
SECOND_CHUNK = {0: (0, 1, 2), 1: (3, 4), 2: (5, 6), 3: (7,)}
LAG_T = 3
LAG_Q = 4
H_SLOTS = 4


def graph_net(nc, x, adj, W1, b1, gamma, beta, W2, b2, WL, out):
    B, C, D = x.shape
    DH = W1.shape[0]
    NT = C // P
    ND = D // P
    NH = DH // P
    CH = 512
    NCH = C // CH
    assert NCH == 2 and NT == 8 and ND == 2 and NH == 4
    DP = D + 2
    YP = 2 * D + 1

    setup_fills = [1, 0, 0, 0, 0, 0, 3, 3]
    setup_empties = [1, 1, 1, 1, 1, 1, 3, 3]
    bank_of, nth = {}, {}
    fills = [0] * N_BANKS
    turn = [0]

    def add_job(stage, tile):
        if stage in PRODUCT_BANKS:
            bank = PRODUCT_BANKS[stage][tile]
        else:
            bank = TRANSPOSE_BANKS[turn[0] % 2]
            turn[0] += 1
        bank_of[stage, tile] = bank
        nth[stage, tile] = fills[bank]
        fills[bank] += 1

    for e in range(NT):
        add_job("S1", e)
        add_job("TA", 2 * e)
        add_job("TA", 2 * e + 1)
    for j in range(NCH * ND):
        add_job("S2", j)
    for s in range(NT + LAG_Q):
        if s < NT:
            add_job("P", s)
        if 0 <= s - LAG_T < NT:
            add_job("TH", s - LAG_T)
        if 0 <= s - LAG_Q < NT:
            add_job("Q", s - LAG_Q)
    for stage in ("S3", "S4"):
        for e in range(NT):
            add_job(stage, e)
    for i in range(NT + 1):
        if i < NT:
            add_job("TX", i)
        if i > 0:
            add_job("V", i - 1)
    for i in range(NT):
        add_job("L", i)

    ctx = ExitStack()
    with ctx:
        at = [(nc.sbuf_base + 63) // 64 * 64]

        def place(name, shape, dt, offset=None):
            n = 4 if dt != BF16 else 2
            for d in shape[1:]:
                n *= d
            if offset is None:
                offset = at[0]
                at[0] += (n + 63) // 64 * 64
            return nc.alloc_sbuf_tensor_at(name, shape, dt, offset=offset), offset, offset + (n + 63) // 64 * 64

        raw, raw_at, _ = place("raw", [P, NT, C], F32)
        H, _, _ = place("H", [P, NT, C], F32R)
        adjT, adjT_at, _ = place("adjT", [P, NT, C], F32)
        HT, HT_at, _ = place("HT", [P, NT, C], F32R)
        x_hi, _, _ = place("x_hi", [P, NT, DP], F32R)
        x_lo, _, _ = place("x_lo", [P, NT, D], F32R)
        m_hi, _, _ = place("m_hi", [P, NT, D], F32R)
        m_lo, _, _ = place("m_lo", [P, NT, D], F32R)
        x_in, _, _ = place("x_in", [P, NT, D], F32)
        xres, _, _ = place("xres", [P, NT, D], F32)
        w_row, _, _ = place("w_row", [P, C], F32)
        W1T, _, _ = place("W1T", [P, ND, DH], F32)
        gW2T, _, _ = place("gW2T", [P, NH, D], F32)
        WLT, _, _ = place("WLT", [P, ND, 2 * D], F32)
        b1_row, _, _ = place("b1_row", [P, DH], F32)
        b2_row, _, _ = place("b2_row", [P, D], F32)
        bW2_row, _, _ = place("bW2_row", [P, D], F32)
        x1T, _, _ = place("x1T", [P, 2, ND, P], F32)
        q_f32, q_at, _ = place("q_f32", [P, 2, D], F32)
        o_f32, _, _ = place("o_f32", [P, 2, D], F32)
        ident, _, _ = place("ident", [P, P], F32)
        small, _, _ = place("small", [P, 20, NT], F32)
        zT, _, nxt = place("zT", [P, ND, C], F32, raw_at)
        hrow, _, nxt = place("hrow", [P, H_SLOTS, DH], F32, nxt)
        xnT, _, _ = place("xnT", [P, 2, NH, P], F32, nxt)
        yv, _, _ = place("yv", [P, NT, YP], F32, HT_at)
        unread, _, _ = place("unread", [P, C], F32, q_at)
        W1n, _, nxt = place("W1n", [P, NH, D], F32, adjT_at)
        W2n, _, nxt = place("W2n", [P, ND, DH], F32, nxt)
        WLn, _, nxt = place("WLn", [P, ND, 2 * D], F32, nxt)
        W2T, _, nxt = place("W2T", [P, NH, D], F32, nxt)
        beta_wide, _, _ = place("beta_wide", [P, NH, P], F32, nxt)

        def col(n):
            return small[:, n, :]

        (dn, dn_pos, dn_safe, dn_inv, rDn, be_safe, rBe, deg_safe, rdeg, std_h, rstd_h, std_1, rstd_1,
         std_o, rstd_o, gb) = (col(n) for n in range(16))
        gamma_c, beta_c, eps_c = gb[:, 0:NH], gb[:, NH:2 * NH], small[:, 16, 0:1]
        stats, _, _ = place("stats", [P, 3, NT, 6], F32)
        mv, _, _ = place("mv", [P, 3, NT, 2], F32)
        assert NT >= 2 * NH and at[0] <= nc.sbuf_usable_end, (at[0], nc.sbuf_usable_end)

        banks = [ctx.enter_context(nc.psum_tensor(f"bank{n}", [P, 512], F32)) for n in range(N_BANKS)]

        def sem(name):
            return ctx.enter_context(nc.semaphore(name))

        bank_full = [sem(f"bank_full{n}") for n in range(N_BANKS)]
        bank_empty = [sem(f"bank_empty{n}") for n in range(N_BANKS)]
        raw_loaded = [sem(f"raw_loaded{n}") for n in range(NT // 2)]
        x_loaded, w_loaded, W2_loaded, W1_loaded, WL_loaded, rows_loaded, bias_loaded, table_loaded = (
            sem(n) for n in ("x_loaded", "w_loaded", "W2_loaded", "W1_loaded", "WL_loaded",
                              "rows_loaded", "bias_loaded",
                              "table_loaded"))
        ident_zero, ident_ready, eps_ready, ones_ready, x_split, x_hi_done, xb_part, xb_ready = (
            sem(n) for n in ("ident_zero", "ident_ready", "eps_ready", "ones_ready", "x_split", "x_hi_done",
                             "xb_part", "xb_ready"))
        q_hi_done, q_split, y_ones = (sem(n) for n in ("q_hi_done", "q_split", "y_ones"))
        H_ready, HT_ready, dn_ready, rDn_part, rDn_ready = (
            sem(n) for n in ("H_ready", "HT_ready", "dn_ready", "rDn_part", "rDn_ready"))
        be_done, rBe_ready, m_hi_done = (sem(n) for n in ("be_done", "rBe_ready", "m_hi_done"))
        relu_done = sem("relu_done")
        deg_done, rdeg_done, o_done, sum_done = (sem(n) for n in ("deg_done", "rdeg_done", "o_done", "sum_done"))
        norms = ("h", "1", "o")
        stats_done = sem("stats_done")
        var_done = {n: sem(f"var_done_{n}") for n in norms}
        std_done = {n: sem(f"std_done_{n}") for n in norms}
        rstd_done = {n: sem(f"rstd_done_{n}") for n in norms}
        normed = {n: sem(f"normed_{n}") for n in norms}
        W2T_scaled, beta_wide_done = sem("W2T_scaled"), sem("beta_wide_done")
        out_stored = sem("out_stored")

        def bank(stage, tile):
            return banks[bank_of[stage, tile]]

        def full(stage, tile, b):
            n = bank_of[stage, tile]
            return bank_full[n], b * fills[n] + (setup_fills[n] + nth[stage, tile] + 1)

        def emptied(stage, tile, b):
            n = bank_of[stage, tile]
            return bank_empty[n], b * fills[n] + (setup_empties[n] + nth[stage, tile] + 1)

        def free(stage, tile, b):
            n = bank_of[stage, tile]
            return bank_empty[n], b * fills[n] + (setup_empties[n] + nth[stage, tile])

        def fills_bank(ins, stage, tile):
            ins.then_inc(bank_full[bank_of[stage, tile]], 1)

        def empties_bank(ins, stage, tile):
            ins.then_inc(bank_empty[bank_of[stage, tile]], 1)

        def over_graphs(eng, graph):
            with eng.Fori(0, B - 1) as b:
                graph(b, True)
            graph(B - 1, False)

        block = ctx.enter_context(nc.Block())

        @block.sync
        def _(sp):
            def load_graph(b, with_w=False):
                for j in range(NT // 2):
                    if j == 1 and with_w:
                        load_w(b)
                    sp.dma_start(raw[:, 2 * j:2 * j + 2, :],
                                 adj[b, 2 * j * P:(2 * j + 2) * P, :].rearrange("(t p) e -> p t e", p=P))\
                      .then_inc(raw_loaded[j], 16)

            def load_x(b):
                sp.dma_start(x_in[:, :, :], x[b, :, :].rearrange("(t p) d -> p t d", p=P)).then_inc(x_loaded, 16)

            def load_w(b):
                sp.dma_start(w_row[:, :], adj[b, 0, :].partition_broadcast(P)).then_inc(w_loaded, 16)

            sp.dma_start(gamma_c, gamma.rearrange("(k p) -> p k", p=P), allow_slow_non_contiguous=True)\
              .then_inc(rows_loaded, 16)
            sp.dma_start(beta_c, beta.rearrange("(k p) -> p k", p=P), allow_slow_non_contiguous=True)\
              .then_inc(rows_loaded, 16)
            sp.dma_start(W2n[:, :, :], W2.rearrange("(t p) d -> p t d", p=P)).then_inc(W2_loaded, 16)
            load_x(0)
            sp.dma_start(W1n[:, :, :], W1.rearrange("(t p) d -> p t d", p=P)).then_inc(W1_loaded, 16)
            sp.dma_start(WLn[:, :, :], WL.rearrange("(t p) d -> p t d", p=P)).then_inc(WL_loaded, 16)
            load_graph(0, with_w=True)
            sp.dma_start(b1_row[:, :], b1.partition_broadcast(P)).then_inc(bias_loaded, 16)
            sp.dma_start(b2_row[:, :], b2.partition_broadcast(P)).then_inc(bias_loaded, 16)

            def graph(b, more):
                if more:
                    sp.wait_ge(dn_ready, b * NT + NT)
                    load_w(b + 1)
                    sp.wait_ge(xb_ready, b + 1)
                    sp.wait_ge(x_split, b + 1)
                    load_x(b + 1)
                    sp.wait_ge(*full("Q", NT - 1, b))
                    load_graph(b + 1)
                for j in range(NT // 2):
                    sp.wait_ge(normed["o"], b * NT + 2 * j + 2)
                    sp.dma_start(out[b, 2 * j * P:(2 * j + 2) * P, :].rearrange("(t p) d -> p t d", p=P),
                                 xres[:, 2 * j:2 * j + 2, :]).then_inc(out_stored, 16)

            over_graphs(sp, graph)
            sp.wait_ge(out_stored, 16 * (NT // 2) * B)

        @block.gpsimd
        def _(pool):
            nc.gpsimd.memset(ident[:, :], 0.0).then_inc(ident_zero, 1)
            nc.gpsimd.memset(x_hi[:, :, D:DP].bitcast(F32), 1.0).then_inc(ones_ready, 1)
            nc.gpsimd.memset(eps_c, NORM_EPS).then_inc(eps_ready, 1)
            pool.wait_ge(ident_zero, 1)
            nc.gpsimd.affine_select(out=ident[:, :], in_=ident[:, :], compare_op=ALU.not_equal, fill=1.0,
                                    base=0, pattern=[[-1, P]], channel_multiplier=1).then_inc(ident_ready, 1)

            def split_x(b):
                pool.wait_ge(x_hi_done, b + 1)
                nc.gpsimd.tensor_tensor(x_lo[:, :, :], x_in[:, :, :], x_hi[:, :, 0:D].bitcast(F32), ALU.subtract)\
                  .then_inc(x_split, 1)

            pool.wait_ge(x_loaded, 16)
            pool.wait_ge(bias_loaded, 16 * 2)

            def residual(b):
                nc.gpsimd.tensor_tensor(xres[:, :, :], x_in[:, :, :], x_in[:, :, :], ALU.add).then_inc(xb_part, 1)
                pool.wait_ge(xb_part, b + 1)
                nc.gpsimd.tensor_tensor(xres[:, :, :], xres[:, :, :],
                                        b2_row[:, :].unsqueeze(1).to_broadcast([P, NT, D]), ALU.add)\
                  .then_inc(xb_ready, 1)

            residual(0)

            def graph(b, more):
                for i in range(NT):
                    pool.wait_ge(q_hi_done, b * NT + i + 1)
                    nc.gpsimd.tensor_tensor(x_lo[:, i, :], q_f32[:, i % 2, :], x_hi[:, i, 0:D].bitcast(F32),
                                            ALU.subtract).then_inc(q_split, 1)
                if more:
                    split_x(b + 1)
                    pool.wait_ge(out_stored, b * (16 * (NT // 2)) + 16 * (NT // 2))
                    residual(b + 1)

            over_graphs(pool, graph)

        @block.scalar
        def _(act):
            act.wait_ge(eps_ready, 1)
            nc.scalar.activation(small[:, 17, 0:1], eps_c, ACT.Sqrt).then_inc(table_loaded, 1)
            def split_x_hi(b):
                act.wait_ge(x_loaded, b * 16 + 16)
                nc.scalar.activation(x_hi[:, :, 0:D], x_in[:, :, :], ACT.Copy).then_inc(x_hi_done, 1)

            targets = [W2T[:, 2 * k:2 * k + 2, :].rearrange("p k o -> p (k o)") for k in range(NH // 2)] + \
                      [W1T[:, d, :] for d in range(ND)] + \
                      [WLT[:, d, :] for d in range(ND)]
            for n, target in enumerate(targets):
                tb = TRANSPOSE_BANKS[n % 2]
                act.wait_ge(bank_full[tb], n // 2 + 1)
                nc.scalar.activation(target, banks[tb][:, :], ACT.Copy).then_inc(bank_empty[tb], 1)
                if n == 1:
                    split_x_hi(0)

            def take_m_hi(stage, e, b, n):
                act.wait_ge(*full(stage, e, b))
                act.wait_ge(rBe_ready, b * NT + (e + 1 if stage == "S1" else NT))
                nc.scalar.activation(m_hi[:, e, :], bank(stage, e)[:, 0:D], ACT.Identity, scale=rBe[:, e:e + 1])\
                  .then_inc(m_hi_done, 1)

            def root(norm, which, std, i, b):
                act.wait_ge(var_done[norm], b * NT + i + 1)
                nc.scalar.activation(std[:, i:i + 1], mv[:, which, i, 1:2], ACT.Sqrt, bias=eps_c)\
                  .then_inc(std_done[norm], 1)

            def take_adjT(c, b):
                for half in range(2):
                    job = 2 * c + half
                    act.wait_ge(*full("TA", job, b))
                    empties_bank(nc.scalar.activation(
                        adjT[:, half * 4:half * 4 + 4, c * P:(c + 1) * P],
                        bank("TA", job)[:, :].rearrange("p (k c) -> p k c", c=P), ACT.Copy), "TA", job)

            for c in range(NT - 1):
                take_adjT(c, 0)
            take_m_hi("S1", 0, 0, 0)
            take_m_hi("S1", 1, 0, 1)
            take_adjT(NT - 1, 0)
            for e in range(2, NT):
                take_m_hi("S1", e, 0, e)

            def graph(b, more):
                def take_zT(ch):
                    for d in range(ND):
                        act.wait_ge(*full("S2", ch * ND + d, b))
                        act.wait_ge(dn_ready, b * NT + ND)
                        empties_bank(nc.scalar.activation(zT[:, d, ch * CH:(ch + 1) * CH],
                                                          bank("S2", ch * ND + d)[:, :], ACT.Copy), "S2", ch * ND + d)

                take_zT(0)
                for s in range(NT + LAG_Q):
                    if s < NT:
                        act.wait_ge(*emptied("P", s, b))
                        nc.scalar.activation(hrow[:, s % H_SLOTS, :], hrow[:, s % H_SLOTS, :], ACT.Relu)\
                          .then_inc(relu_done, 1)
                    if s == max(SECOND_CHUNK) - 1:
                        take_zT(1)
                    if 0 <= s - LAG_T < NT:
                        i = s - LAG_T
                        act.wait_ge(*full("TH", i, b))
                        empties_bank(nc.scalar.activation(xnT[:, i % 2, :, :].rearrange("p k c -> p (k c)"),
                                                          bank("TH", i)[:, :], ACT.Copy), "TH", i)
                    if s < NT:
                        root("h", 0, std_h, s, b)
                    if s >= LAG_Q:
                        i = s - LAG_Q
                        act.wait_ge(*emptied("Q", i, b))
                        nc.scalar.activation(x_hi[:, i, 0:D], q_f32[:, i % 2, :], ACT.Copy).then_inc(q_hi_done, 1)
                for e in range(NT):
                    take_m_hi("S3", e, b, NT + e)
                if more:
                    split_x_hi(b + 1)
                def take_x1T(i):
                    act.wait_ge(*full("TX", i, b))
                    empties_bank(nc.scalar.activation(x1T[:, i % 2, :, :].rearrange("p k c -> p (k c)"),
                                                      bank("TX", i)[:, 0:D], ACT.Copy), "TX", i)

                for i in range(NT - 2):
                    root("1", 1, std_1, i, b)
                take_x1T(0)
                take_x1T(1)
                root("1", 1, std_1, NT - 2, b)
                root("1", 1, std_1, NT - 1, b)
                for i in range(NT):
                    act.wait_ge(*full("V", i, b))
                    empties_bank(nc.scalar.activation(yv[:, i, 0:2 * D], bank("V", i)[:, :], ACT.Copy), "V", i)
                    if i + 2 < NT:
                        take_x1T(i + 2)
                for i in range(NT):
                    root("o", 2, std_o, i, b)
                if more:
                    for e in range(NT):
                        take_adjT(e, b + 1)
                        take_m_hi("S1", e, b + 1, e)

            over_graphs(act, graph)

        @block.vector
        def _(dve):
            def build_H_tile(c, b):
                dve.wait_ge(raw_loaded[c // 2], b * 16 + 16)
                nc.vector.tensor_scalar(H[:, c, :], raw[:, c, :], 0.0, None, ALU.not_equal).then_inc(H_ready, 1)

            def sum_Dn(c, b):
                if c == 0:
                    dve.wait_ge(w_loaded, b * 16 + 16)
                else:
                    dve.wait_ge(dn_ready, b * NT + c)
                nc.vector.scalar_tensor_tensor(out=unread[:, :], in0=raw[:, c, :], scalar=0.0, in1=w_row[:, :],
                                               op0=ALU.not_equal, op1=ALU.mult,
                                               accum_out=dn[:, c:c + 1]).then_inc(dn_ready, 1)

            def build_rDn(b):
                dve.wait_ge(dn_ready, b * NT + NT)
                nc.vector.tensor_scalar(dn_pos, dn, 0.0, None, ALU.is_gt).then_inc(rDn_part, 1)
                nc.vector.tensor_scalar(dn_safe, dn, TINY, None, ALU.max).then_inc(rDn_part, 1)
                dve.wait_ge(rDn_part, b * 3 + 2)
                nc.vector.reciprocal(dn_inv, dn_safe).then_inc(rDn_part, 1)
                dve.wait_ge(rDn_part, b * 3 + 3)
                nc.vector.tensor_tensor(rDn, dn_inv, dn_pos, ALU.mult).then_inc(rDn_ready, 1)

            def inverse_root(norm, std, rstd, i, b):
                dve.wait_ge(std_done[norm], b * NT + i + 1)
                nc.vector.reciprocal(rstd[:, i:i + 1], std[:, i:i + 1]).then_inc(rstd_done[norm], 1)

            def centre(norm, which, rows, rstd, i, b):
                dve.wait_ge(rstd_done[norm], b * NT + i + 1)
                nc.vector.tensor_scalar(rows, rows, mv[:, which, i, 0:1], rstd[:, i:i + 1],
                                        ALU.subtract, ALU.mult).then_inc(normed[norm], 1)

            def moments(norm, which, src, i, b):
                nc.vector.bn_stats(stats[:, which, i, :], src)
                dve.drain()
                nc.vector.bn_aggr(mv[:, which, i, :], stats[:, which, i, :]).then_inc(var_done[norm], 1)

            def take_m_lo(stage, e, b, n):
                dve.wait_ge(m_hi_done, b * (2 * NT) + (n + 1))
                empties_bank(nc.vector.scalar_tensor_tensor(
                    out=m_lo[:, e, :], in0=bank(stage, e)[:, 0:D], scalar=rBe[:, e:e + 1],
                    in1=m_hi[:, e, :].bitcast(F32), op0=ALU.mult, op1=ALU.subtract), stage, e)

            def build_HT(c, b):
                dve.wait_ge(*emptied("TA", 2 * c, b))
                dve.wait_ge(*emptied("TA", 2 * c + 1, b))
                nc.vector.tensor_scalar(HT[:, :, c * P:(c + 1) * P], adjT[:, :, c * P:(c + 1) * P], 0.0, None,
                                        ALU.not_equal).then_inc(HT_ready, 1)

            for n in range(1, TRANSPOSE_BANKS[0]):
                nc.vector.memset(banks[n][:, 0:1], 0.0).then_inc(bank_empty[n], 1)
            dve.wait_ge(rows_loaded, 16 * 2)
            for k in range(NH):
                nc.vector.tensor_copy(beta_wide[:, k, :], beta_c[:, k:k + 1].to_broadcast([P, P]))\
                  .then_inc(beta_wide_done, 1)
            for n in range(NH // 2):
                tb = TRANSPOSE_BANKS[n % 2]
                dve.wait_ge(bank_empty[tb], n // 2 + 1)
                for k in (2 * n, 2 * n + 1):
                    nc.vector.tensor_scalar(gW2T[:, k, :], W2T[:, k, :], gamma_c[:, k:k + 1], None, ALU.mult)\
                      .then_inc(W2T_scaled, 1)

            def take_rBe(e, b):
                dve.wait_ge(*full("S1", e, b))
                nc.vector.tensor_scalar(be_safe[:, e:e + 1], bank("S1", e)[:, D:D + 1], 1.0, None, ALU.max)\
                  .then_inc(be_done, 1)
                dve.wait_ge(be_done, b * NT + e + 1)
                nc.vector.reciprocal(rBe[:, e:e + 1], be_safe[:, e:e + 1]).then_inc(rBe_ready, 1)

            dve.wait_ge(x_hi_done, 1)
            nc.vector.tensor_tensor(x_lo[:, :, :], x_in[:, :, :], x_hi[:, :, 0:D].bitcast(F32), ALU.subtract)\
              .then_inc(x_split, 1)
            dve.wait_ge(bank_full[0], 1)
            nc.vector.tensor_copy(bW2_row[:, :], banks[0][:, 0:D]).then_inc(bank_empty[0], 1)
            for c in range(NT):
                build_H_tile(c, 0)
                sum_Dn(c, 0)
                if c >= 2:
                    build_HT(c - 2, 0)
            build_HT(NT - 2, 0)
            n_side = TRANSPOSE_BANKS[0]
            take_rBe(0, 0)
            for e in range(NT):
                if e == 2:
                    build_HT(NT - 1, 0)
                if e + 1 < n_side:
                    take_rBe(e + 1, 0)
                take_m_lo("S1", e, 0, e)
                if n_side <= e + 1 < NT:
                    take_rBe(e + 1, 0)
            build_rDn(0)

            def graph(b, more):
                dve.wait_ge(bias_loaded, 16 * 2)
                dve.wait_ge(rDn_ready, b + 1)
                for s in range(NT + LAG_Q):
                    if s < NT:
                        dve.wait_ge(*full("P", s, b))
                        empties_bank(nc.vector.scalar_tensor_tensor(
                            out=hrow[:, s % H_SLOTS, :], in0=bank("P", s)[:, :], scalar=rDn[:, s:s + 1],
                            in1=b1_row[:, :], op0=ALU.mult, op1=ALU.add), "P", s)
                    if 0 <= s - 1 < NT:
                        inverse_root("h", std_h, rstd_h, s - 1, b)
                        centre("h", 0, hrow[:, (s - 1) % H_SLOTS, :], rstd_h, s - 1, b)
                    if s < NT:
                        dve.wait_ge(relu_done, b * NT + s + 1)
                        moments("h", 0, hrow[:, s % H_SLOTS, :], s, b)
                    if s >= LAG_Q:
                        i = s - LAG_Q
                        dve.wait_ge(*full("Q", i, b))
                        if i >= 2:
                            dve.wait_ge(q_split, b * NT + i - 1)
                        empties_bank(nc.vector.tensor_tensor(q_f32[:, i % 2, :], bank("Q", i)[:, 0:D],
                                                             bW2_row[:, :], ALU.add), "Q", i)
                for e in range(NT):
                    take_m_lo("S3", e, b, NT + e)

                dve.wait_ge(xb_ready, b + 1)
                for i in range(NT + 1):
                    if i < NT:
                        dve.wait_ge(*full("S4", i, b))
                        empties_bank(nc.vector.scalar_tensor_tensor(
                            out=xres[:, i, :], in0=bank("S4", i)[:, 0:D], scalar=rDn[:, i:i + 1],
                            in1=xres[:, i, :], op0=ALU.mult, op1=ALU.add), "S4", i)
                    if i > 0:
                        inverse_root("1", std_1, rstd_1, i - 1, b)
                    if i < NT:
                        dve.wait_ge(*emptied("S4", i, b))
                        nc.vector.bn_stats(stats[:, 1, i, :], xres[:, i, :]).then_inc(stats_done, 1)
                    if i > 0:
                        if i < NT:
                            dve.wait_ge(stats_done, b * NT + i + 1)
                        centre("1", 1, xres[:, i - 1, :], rstd_1, i - 1, b)
                    if i < NT:
                        if i == 0:
                            dve.drain()
                        nc.vector.bn_aggr(mv[:, 1, i, :], stats[:, 1, i, :]).then_inc(var_done["1"], 1)
                nc.vector.memset(yv[:, :, 2 * D:YP], 1.0).then_inc(y_ones, 1)
                if more:
                    for c in range(NT):
                        build_H_tile(c, b + 1)
                for i in range(NT + 1):
                    if i < NT:
                        dve.wait_ge(*full("L", i, b))
                        nc.vector.tensor_scalar(deg_safe[:, i:i + 1], bank("L", i)[:, D:D + 1], DEG_EPS, None,
                                                ALU.max).then_inc(deg_done, 1)
                    if i > 0:
                        inverse_root("o", std_o, rstd_o, i - 1, b)
                    if i < NT:
                        dve.wait_ge(deg_done, b * NT + i + 1)
                        nc.vector.reciprocal(rdeg[:, i:i + 1], deg_safe[:, i:i + 1]).then_inc(rdeg_done, 1)
                    if i > 0:
                        centre("o", 2, xres[:, i - 1, :], rstd_o, i - 1, b)
                    if i < NT:
                        dve.wait_ge(rdeg_done, b * NT + i + 1)
                        empties_bank(nc.vector.scalar_tensor_tensor(
                            out=o_f32[:, i % 2, :], in0=bank("L", i)[:, 0:D], scalar=rdeg[:, i:i + 1],
                            in1=yv[:, i, 0:D], op0=ALU.mult, op1=ALU.add), "L", i)
                        dve.wait_ge(*emptied("L", i, b))
                        nc.vector.scalar_tensor_tensor(out=xres[:, i, :], in0=o_f32[:, i % 2, :], scalar=0.0,
                                                       in1=xres[:, i, :], op0=ALU.max, op1=ALU.add)\
                          .then_inc(sum_done, 1)
                        dve.wait_ge(sum_done, b * NT + i + 1)
                        moments("o", 2, xres[:, i, :], i, b)
                if more:
                    for e in range(NT):
                        take_rBe(e, b + 1)
                        if e > 0:
                            build_HT(e - 1, b + 1)
                        take_m_lo("S1", e, b + 1, e)
                    build_HT(NT - 1, b + 1)
                    for c in range(NT):
                        sum_Dn(c, b + 1)
                    build_rDn(b + 1)

            over_graphs(dve, graph)

        @block.tensor
        def _(pe):
            mm = nc.tensor.matmul

            pe.wait_ge(ident_ready, 1)
            fours = [[W2n[:, o, k * P:(k + 1) * P] for k in (2 * n, 2 * n + 1) for o in range(ND)]
                     for n in range(NH // 2)] + \
                    [[W1n[:, h, d * P:(d + 1) * P] for h in range(NH)] for d in range(ND)] + \
                    [[WLn[:, o, (side * ND + d) * P:(side * ND + d + 1) * P] for side in range(2) for o in range(ND)]
                     for d in range(ND)]
            loads = (W2_loaded, W1_loaded, WL_loaded)
            for n, four in enumerate(fours):
                tb = TRANSPOSE_BANKS[n % 2]
                if n % 2 == 0:
                    pe.wait_ge(loads[n // 2], 16)
                if n >= 2:
                    pe.wait_ge(bank_empty[tb], n // 2)
                if n == 4:
                    pe.wait_ge(bank_empty[TRANSPOSE_BANKS[1]], 1)
                    pe.wait_ge(beta_wide_done, NH)
                    for k in range(NH):
                        last = mm(banks[0][:, 0:D], beta_wide[:, k, :], W2T[:, k, :],
                                  start=(k == 0), stop=(k == NH - 1))
                    last.then_inc(bank_full[0], 1)
                for j, src in enumerate(four):
                    last = nc.tensor.transpose(banks[tb][:, j * P:(j + 1) * P], src, ident[:, :])
                last.then_inc(bank_full[tb], 1)
            pe.wait_ge(W2T_scaled, NH)
            pe.wait_ge(ones_ready, 1)

            def tiled(stage, b, n_cols, ready, parts, operands, before_last=None):
                def one(i, k):
                    for part in range(parts):
                        lhsT, rhs = operands(k, i, part)
                        last = mm(bank(stage, i)[:, 0:n_cols], lhsT, rhs, start=(k == 0 and part == 0),
                                  stop=(k == NT - 1 and part == parts - 1))
                    if k == NT - 1:
                        fills_bank(last, stage, i)

                for k in range(NT):
                    ready(k)
                    for i in range(GROUP):
                        if k == 0:
                            pe.wait_ge(*free(stage, i, b))
                        one(i, k)
                for i in range(GROUP, NT):
                    if i == NT - 1 and before_last:
                        before_last()
                    pe.wait_ge(*free(stage, i, b))
                    for k in range(NT):
                        one(i, k)

            def s1_step(e, c, b):
                lhsT = H[:, c, e * P:(e + 1) * P]
                hi = (bank("S1", e)[:, 0:DP], lhsT, x_hi[:, c, :])
                lo = (bank("S1", e)[:, 0:D], lhsT, x_lo[:, c, :])
                for n, args in enumerate((hi, lo) if c < NT - 1 else (lo, hi)):
                    last = mm(*args, start=(c == 0 and n == 0), stop=(c == NT - 1 and n == 1))
                if c == NT - 1:
                    fills_bank(last, "S1", e)

            def transpose_adj(c, b):
                for job in (2 * c, 2 * c + 1):
                    pe.wait_ge(*free("TA", job, b))
                    for k in range(4):
                        kt = job % 2 * 4 + k
                        last = nc.tensor.transpose(bank("TA", job)[:, k * P:(k + 1) * P],
                                                   raw[:, c, kt * P:(kt + 1) * P], ident[:, :])
                    fills_bank(last, "TA", job)

            n_side = TRANSPOSE_BANKS[0]
            pe.wait_ge(x_split, 1)
            for c in range(NT):
                pe.wait_ge(H_ready, c + 1)
                for e in range(n_side):
                    if c == 0:
                        pe.wait_ge(*free("S1", e, 0))
                    s1_step(e, c, 0)
                transpose_adj(c, 0)
            for e in range(n_side, NT):
                pe.wait_ge(*free("S1", e, 0))
                for c in range(NT):
                    s1_step(e, c, 0)

            def graph(b, more):
                def s2_step(ch, k):
                    for d in range(ND):
                        job = ch * ND + d
                        if k == 0:
                            pe.wait_ge(*free("S2", job, b))
                        for n, m in enumerate((m_hi, m_lo)):
                            last = mm(bank("S2", job)[:, :], m[:, k, d * P:(d + 1) * P],
                                      HT[:, k, ch * CH:(ch + 1) * CH], start=(k == 0 and n == 0),
                                      stop=(k == NT - 1 and n == 1))
                        if k == NT - 1:
                            fills_bank(last, "S2", job)

                pe.wait_ge(HT_ready, b * NT + NT // NCH)
                for k in range(NT):
                    pe.wait_ge(*emptied("S1", k, b))
                    s2_step(0, k)
                pe.wait_ge(HT_ready, b * NT + NT)
                for s in range(NT + LAG_Q):
                    for k in SECOND_CHUNK.get(s, ()):
                        s2_step(1, k)
                    if s < NT:
                        pe.wait_ge(*free("P", s, b))
                        if s % (CH // P) == 0:
                            for d in range(ND):
                                pe.wait_ge(*emptied("S2", s // (CH // P) * ND + d, b))
                        for d in range(ND):
                            last = mm(bank("P", s)[:, :], zT[:, d, s * P:(s + 1) * P], W1T[:, d, :],
                                      start=(d == 0), stop=(d == ND - 1))
                        fills_bank(last, "P", s)
                    i = s - LAG_T
                    if 0 <= i < NT:
                        pe.wait_ge(*free("TH", i, b))
                        pe.wait_ge(normed["h"], b * NT + i + 1)
                        for k in range(NH):
                            last = nc.tensor.transpose(bank("TH", i)[:, k * P:(k + 1) * P],
                                                       hrow[:, i % H_SLOTS, k * P:(k + 1) * P], ident[:, :])
                        fills_bank(last, "TH", i)
                    i = s - LAG_Q
                    if 0 <= i < NT:
                        pe.wait_ge(*free("Q", i, b))
                        pe.wait_ge(*emptied("TH", i, b))
                        for k in range(NH):
                            last = mm(bank("Q", i)[:, 0:D], xnT[:, i % 2, k, :], gW2T[:, k, :],
                                      start=(k == 0), stop=(k == NH - 1))
                        fills_bank(last, "Q", i)

                def transpose_x1(i):
                    pe.wait_ge(*free("TX", i, b))
                    pe.wait_ge(normed["1"], b * NT + i + 1)
                    for d in range(ND):
                        last = nc.tensor.transpose(bank("TX", i)[:, d * P:(d + 1) * P],
                                                   xres[:, i, d * P:(d + 1) * P], ident[:, :])
                    fills_bank(last, "TX", i)

                tiled("S3", b, D, lambda c: pe.wait_ge(q_split, b * NT + c + 1), 2,
                      lambda c, e, part: (H[:, c, e * P:(e + 1) * P], (x_hi, x_lo)[part][:, c, 0:D]))
                tiled("S4", b, D, lambda e: pe.wait_ge(*emptied("S3", e, b)), 2,
                      lambda e, i, part: (HT[:, e, i * P:(i + 1) * P], (m_hi, m_lo)[part][:, e, :]),
                      before_last=lambda: (transpose_x1(0), transpose_x1(1)))

                for i in range(NT):
                    pe.wait_ge(*free("V", i, b))
                    pe.wait_ge(*emptied("TX", i, b))
                    for d in range(ND):
                        last = mm(bank("V", i)[:, :], x1T[:, i % 2, d, :], WLT[:, d, :],
                                  start=(d == 0), stop=(d == ND - 1))
                    fills_bank(last, "V", i)
                    if i + 2 < NT:
                        transpose_x1(i + 2)

                pe.wait_ge(y_ones, b + 1)
                tiled("L", b, D + 1, lambda j: pe.wait_ge(*emptied("V", j, b)), 1,
                      lambda j, i, part: (adjT[:, j, i * P:(i + 1) * P], yv[:, j, D:YP]))

                if more:
                    pe.wait_ge(x_split, b + 2)
                    for e in range(NT):
                        pe.wait_ge(*free("S1", e, b + 1))
                        for c in range(NT):
                            if e == 0:
                                pe.wait_ge(H_ready, (b + 1) * NT + c + 1)
                            s1_step(e, c, b + 1)
                        transpose_adj(e, b + 1)

            over_graphs(pe, graph)


_INS = ['x', 'adj', 'L0_gnn_W1', 'L0_gnn_b1', 'L0_gnn_gamma', 'L0_gnn_beta', 'L0_gnn_W2', 'L0_gnn_b2', 'L1_gnn_W']


def kernel(**inputs):
    import numpy as _np
    import concourse.bacc as _bacc
    from concourse import mybir as _mybir
    from concourse.bass_utils import run_bass_kernel_spmd as _run

    nc = _bacc.Bacc("TRN2", target_bir_lowering=False, num_devices=1)
    arrays, args = {}, []
    for name in _INS:
        a = _np.ascontiguousarray(inputs[name])
        arrays[f"in_{name}_dram"] = a
        args.append(nc.dram_tensor(f"in_{name}_dram", a.shape, _mybir.dt.from_np(a.dtype), kind="ExternalInput").ap())
    shape = inputs['x'].shape
    args.append(nc.dram_tensor("out_0_dram", shape, _mybir.dt.from_np(_np.dtype('float32')),
                               kind="ExternalOutput").ap())
    graph_net(nc, *args)
    r = _run(nc, [arrays], core_ids=[0])
    return r.results[0]["out_0_dram"]
```
